# Optimizing a Trainium2 kernel written in Bass

```python
import numpy as np
import jax
import jax.numpy as jnp

def _softmax(x, axis=-1):
    return jax.nn.softmax(x, axis=axis)

def _gelu(x):
    return jax.nn.gelu(x, approximate=True)

def _silu(x):
    return jax.nn.silu(x)

def _sigmoid(x):
    return jax.nn.sigmoid(x)

def _layernorm(x, axis=-1, eps=1e-05):
    m = jnp.mean(x, axis=axis, keepdims=True)
    v = jnp.var(x, axis=axis, keepdims=True)
    return (x - m) / jnp.sqrt(v + eps)

def _scatter_add(tgt, idx, src, axis=0):
    return tgt.at[idx].add(src)

def _segment_sum(src, seg, n):
    return jax.ops.segment_sum(src, seg, n)
kernel_name = 'mk_decoder_postln_d1_seqx_r8_bbb4d6'

def setup_inputs(seed: int=0):
    np.random.seed(seed)
    _w = jnp.asarray

    def _rec_inputs():
        import jax
        import jax.numpy as jnp
        _rk = jax.random.key(seed)
        x = -0.0003929 + 0.9999 * jax.random.normal(jax.random.fold_in(_rk, 1), (16, 128, 128), jnp.float32)
        _lenS = 128 - jax.random.randint(jax.random.fold_in(_rk, 7), (16,), 0, max(1, 128 // 4) + 1, jnp.int32)
        _lenS2 = 128 - jax.random.randint(jax.random.fold_in(_rk, 8), (16,), 0, max(1, 128 // 4) + 1, jnp.int32)
        _ctx_1024P = jax.random.normal(jax.random.fold_in(_rk, 11), (16, 16, 128), jnp.float32)
        _ctx_1024c = jax.random.dirichlet(jax.random.fold_in(_rk, 511), 0.3 * jnp.ones((16,), jnp.float32), (16, 128))
        _ctx_1024t = jnp.einsum('bsk,bkd->bsd', _ctx_1024c, _ctx_1024P)
        _ctx_1024t = _ctx_1024t * jax.lax.rsqrt(jnp.mean(jnp.square(_ctx_1024t)) + 1e-12) * 0.953939
        ctx_1024 = 2.81802e-05 + 1.00001 * (_ctx_1024t + 0.3 * jax.random.normal(jax.random.fold_in(_rk, 611), (16, 128, 128), jnp.float32))
        return (x, ctx_1024)
    x, ctx_1024 = _rec_inputs()

    def _L0_attn_setup():
        import jax, jax.numpy as jnp
        import numpy as np
        B, N, D = (4, 256, 128)
        H, HD = (16, 64)
        MAX_SEQ = 512
        INNER = H * HD

        def _rope_tables(n, head_dim):
            inv_freq = 1.0 / 10000.0 ** (jnp.arange(0, head_dim, 2, dtype=jnp.float32) / head_dim)
            pos = jnp.arange(n, dtype=jnp.float32)
            ang = pos[:, None] * inv_freq[None, :]
            return (jnp.sin(ang), jnp.cos(ang))
        key = jax.random.key(seed)
        ks = jax.random.split(key, 5)
        s = 0.02
        return {'x': jax.random.normal(ks[0], (B, N, D), dtype=jnp.float32), 'ln_gamma': jnp.ones((D,), jnp.float32), 'ln_beta': jnp.zeros((D,), jnp.float32), 'w_qkv': jax.random.normal(ks[1], (D, 3 * INNER), dtype=jnp.float32) * s, 'w_out': jax.random.normal(ks[2], (INNER, D), dtype=jnp.float32) * s, 'b_out': jnp.zeros((D,), jnp.float32)}
    _L0_attn_all = _L0_attn_setup()
    _L0_attn_in = {k: v for k, v in _L0_attn_all.items() if k in ('ln_gamma', 'ln_beta', 'w_qkv', 'w_out', 'b_out')}
    del _L0_attn_all

    def _L0_xattn_setup():
        import jax, jax.numpy as jnp
        import numpy as np
        INF = 10000000000.0
        D_KEY = 128
        key = jax.random.key(seed)
        k1, k2, k3 = jax.random.split(key, 3)
        B, S, D = (8, 256, D_KEY)
        return {'query': jax.random.normal(k1, (B, S, D), dtype=jnp.float32), 'key': jax.random.normal(k2, (B, S, D), dtype=jnp.float32), 'value': jax.random.normal(k3, (B, S, D), dtype=jnp.float32)}
    _L0_xattn_all = _L0_xattn_setup()
    _L0_xattn_in = {k: v for k, v in _L0_xattn_all.items() if k in ()}
    del _L0_xattn_all

    def _L0_ffn_setup():
        import jax, jax.numpy as jnp
        import numpy as np
        TOP_K = 2
        TEMP = 0.9
        EPS = 1e-05
        B, S, D, F, E = (2, 256, 128, 512, 8)

        def _moe_forward(x, gate_w, gate_b, w1, b1, w2, b2, ln_g, ln_b):
            logits = (x @ gate_w + gate_b) / TEMP
            topk_vals, topk_idx = jax.lax.top_k(logits, TOP_K)
            keep = jax.nn.one_hot(topk_idx, E, dtype=jnp.bool_).any(-2)
            masked = jnp.where(keep, logits, -jnp.inf)
            gate_probs = jax.nn.softmax(masked, axis=-1)
            h = jnp.einsum('bsd,edf->bsef', x, w1) + b1
            h = jax.nn.gelu(h, approximate=False)
            expert_out = jnp.einsum('bsef,efd->bsed', h, w2) + b2
            out = jnp.einsum('bse,bsed->bsd', gate_probs, expert_out)
            mu = out.mean(-1, keepdims=True)
            var = out.var(-1, keepdims=True)
            out = (out - mu) / jnp.sqrt(var + EPS) * ln_g + ln_b
            return out
        key = jax.random.key(seed)
        ks = jax.random.split(key, 4)
        scale_in = 1.0 / np.sqrt(D)
        scale_ff = 1.0 / np.sqrt(F)
        return {'x': jax.random.normal(ks[0], (B, S, D), jnp.float32), 'gate_w': jax.random.normal(ks[1], (D, E), jnp.float32) * scale_in, 'gate_b': jnp.zeros((E,), jnp.float32), 'w1': jax.random.normal(ks[2], (E, D, F), jnp.float32) * scale_in, 'b1': jnp.zeros((E, F), jnp.float32), 'w2': jax.random.normal(ks[3], (E, F, D), jnp.float32) * scale_ff, 'b2': jnp.zeros((E, D), jnp.float32), 'ln_g': jnp.ones((D,), jnp.float32), 'ln_b': jnp.zeros((D,), jnp.float32)}
    _L0_ffn_all = _L0_ffn_setup()
    _L0_ffn_in = {k: v for k, v in _L0_ffn_all.items() if k in ('gate_w', 'gate_b', 'w1', 'b1', 'w2', 'b2', 'ln_g', 'ln_b')}
    del _L0_ffn_all
    return {'x': x, 'ctx_1024': ctx_1024, 'L0_attn_ln_gamma': _L0_attn_in['ln_gamma'], 'L0_attn_ln_beta': _L0_attn_in['ln_beta'], 'L0_attn_w_qkv': _L0_attn_in['w_qkv'], 'L0_attn_w_out': _L0_attn_in['w_out'], 'L0_attn_b_out': _L0_attn_in['b_out'], 'L0_ffn_gate_w': _L0_ffn_in['gate_w'], 'L0_ffn_gate_b': _L0_ffn_in['gate_b'], 'L0_ffn_w1': _L0_ffn_in['w1'], 'L0_ffn_b1': _L0_ffn_in['b1'], 'L0_ffn_w2': _L0_ffn_in['w2'], 'L0_ffn_b2': _L0_ffn_in['b2'], 'L0_ffn_ln_g': _L0_ffn_in['ln_g'], 'L0_ffn_ln_b': _L0_ffn_in['ln_b']}

def reference(x, ctx_1024, L0_attn_ln_gamma, L0_attn_ln_beta, L0_attn_w_qkv, L0_attn_w_out, L0_attn_b_out, L0_ffn_gate_w, L0_ffn_gate_b, L0_ffn_w1, L0_ffn_b1, L0_ffn_w2, L0_ffn_b2, L0_ffn_ln_g, L0_ffn_ln_b):
    import jax
    import jax.numpy as jnp

    def _L0_attn_ref(x, ln_gamma, ln_beta, w_qkv, w_out, b_out):
        import jax, jax.numpy as jnp
        import numpy as np
        B, N, D = (4, 256, 128)
        H, HD = (16, 64)
        MAX_SEQ = 512
        INNER = H * HD

        def _rope_tables(n, head_dim):
            inv_freq = 1.0 / 10000.0 ** (jnp.arange(0, head_dim, 2, dtype=jnp.float32) / head_dim)
            pos = jnp.arange(n, dtype=jnp.float32)
            ang = pos[:, None] * inv_freq[None, :]
            return (jnp.sin(ang), jnp.cos(ang))
        b, n, d = x.shape
        mu = jnp.mean(x, axis=-1, keepdims=True)
        var = jnp.var(x, axis=-1, keepdims=True)
        xn = (x - mu) / jnp.sqrt(var + 1e-05) * ln_gamma + ln_beta
        qkv = xn @ w_qkv
        q, k, v = jnp.split(qkv, 3, axis=-1)

        def to_heads(t):
            return t.reshape(b, n, H, HD).transpose(0, 2, 1, 3)
        q, k, v = (to_heads(q), to_heads(k), to_heads(v))
        sin, cos = _rope_tables(n, HD)
        sin = sin[None, None]
        cos = cos[None, None]
        half = HD // 2

        def rotate(t):
            t1, t2 = (t[..., :half], t[..., half:])
            return jnp.concatenate([t1 * cos - t2 * sin, t2 * cos + t1 * sin], axis=-1)
        qr, kr = (rotate(q), rotate(k))
        scale = HD ** (-0.5)
        scores = jnp.einsum('bhid,bhjd->bhij', qr, kr) * scale
        probs = jax.nn.softmax(scores, axis=-1)
        out = jnp.einsum('bhij,bhjd->bhid', probs, v)
        out = out.transpose(0, 2, 1, 3).reshape(b, n, INNER)
        return out @ w_out + b_out

    def _L0_xattn_ref(query, key, value):
        import jax, jax.numpy as jnp
        import numpy as np
        INF = 10000000000.0
        D_KEY = 128
        scale = jnp.asarray(np.sqrt(D_KEY), dtype=query.dtype)
        dots = jnp.einsum('bqd,bkd->bqk', query, key)
        S = key.shape[1]
        tri = jnp.triu(jnp.ones((S, S), dtype=dots.dtype), k=1) * INF
        dots = dots - tri[None, :, :]
        attn = jax.nn.softmax(dots / scale, axis=-1)
        return jnp.einsum('bqk,bkd->bqd', attn, value)

    def _L0_ffn_ref(x, gate_w, gate_b, w1, b1, w2, b2, ln_g, ln_b):
        import jax, jax.numpy as jnp
        import numpy as np
        TOP_K = 2
        TEMP = 0.9
        EPS = 1e-05
        B, S, D, F, E = (2, 256, 128, 512, 8)

        def _moe_forward(x, gate_w, gate_b, w1, b1, w2, b2, ln_g, ln_b):
            logits = (x @ gate_w + gate_b) / TEMP
            topk_vals, topk_idx = jax.lax.top_k(logits, TOP_K)
            keep = jax.nn.one_hot(topk_idx, E, dtype=jnp.bool_).any(-2)
            masked = jnp.where(keep, logits, -jnp.inf)
            gate_probs = jax.nn.softmax(masked, axis=-1)
            h = jnp.einsum('bsd,edf->bsef', x, w1) + b1
            h = jax.nn.gelu(h, approximate=False)
            expert_out = jnp.einsum('bsef,efd->bsed', h, w2) + b2
            out = jnp.einsum('bse,bsed->bsd', gate_probs, expert_out)
            mu = out.mean(-1, keepdims=True)
            var = out.var(-1, keepdims=True)
            out = (out - mu) / jnp.sqrt(var + EPS) * ln_g + ln_b
            return out
        return _moe_forward(x, gate_w, gate_b, w1, b1, w2, b2, ln_g, ln_b)
    x = _layernorm(x + _L0_attn_ref(x, L0_attn_ln_gamma, L0_attn_ln_beta, L0_attn_w_qkv, L0_attn_w_out, L0_attn_b_out), axis=-1)
    x = _layernorm(x + _L0_xattn_ref(x, ctx_1024, ctx_1024), axis=-1)
    x = _layernorm(x + _L0_ffn_ref(x, L0_ffn_gate_w, L0_ffn_gate_b, L0_ffn_w1, L0_ffn_b1, L0_ffn_w2, L0_ffn_b2, L0_ffn_ln_g, L0_ffn_ln_b), axis=-1)
    return x

_drawn_inputs = setup_inputs


def setup_inputs(seed=0):
    import zlib

    import numpy as np

    out = dict(_drawn_inputs(seed))
    spreads = {'L0_attn_ln_gamma': (1.0, 0.6),
     'L0_attn_ln_beta': (0.0, 0.1),
     'L0_attn_b_out': (0.0, 0.1),
     'L0_ffn_gate_b': (0.0, 0.1),
     'L0_ffn_b1': (0.0, 0.1),
     'L0_ffn_b2': (0.0, 0.1),
     'L0_ffn_ln_g': (1.0, 0.2),
     'L0_ffn_ln_b': (0.0, 0.1)}
    factors = {}
    for name, (base, spread) in spreads.items():
        noise = np.random.default_rng([zlib.crc32(name.encode()), seed]).standard_normal(out[name].shape)
        drawn = base * np.exp(spread * noise) if base else spread * noise
        out[name] = jnp.asarray(drawn.astype(out[name].dtype))
    for name, factor in factors.items():
        out[name] = (out[name] * factor).astype(out[name].dtype)
    return out
```

```python
from contextlib import ExitStack

import concourse.bass as bass
from concourse import mybir

F32 = mybir.dt.float32
F32R = mybir.dt.float32r
U32 = mybir.dt.uint32
ALU = mybir.AluOpType
ACT = mybir.ActivationFunctionType
AX = mybir.AxisListType

B, N, D = 16, 128, 128
H, HD = 16, 64
PAIRS = H // 2
QUADS = H // 4
E, F = 8, 512
FT = F // 128
CHUNK = 512
BLOCK = 512
NBLOCKS = B * N // BLOCK
TPB = BLOCK // N
WCOLS = E * F // B
EPS = 1e-5
INV_TEMP = 1.0 / 0.9
CROSS_SCALE = float(D) ** -0.5

CHUNKS = [0, 2 * CHUNK, CHUNK, 3 * CHUNK, 4 * CHUNK, 5 * CHUNK]
ROPE_CHUNKS = 4
COS, SIN = 0, 1


def head_of(t, j):
    return 4 * (t // 2) + j, t % 2


def made(count, most):
    return min(count, most) if isinstance(count, int) else count


class Count:

    def __init__(self, register, times=1, plus=0):
        self.register, self.times, self.plus = register, times, plus

    def __add__(self, n):
        return Count(self.register, self.times, self.plus + n)

    def __sub__(self, n):
        return self + -n

    def __mul__(self, n):
        return Count(self.register, self.times * n, self.plus * n)

    __radd__, __rmul__ = __add__, __mul__


def at(n):
    if isinstance(n, int):
        return n
    value = n.register * n.times if n.times != 1 else n.register
    return value + n.plus if n.plus else value


class Turn:

    def __init__(self, i, parity):
        self.i, self.parity, self.b = i, parity, 2 * i + parity

    def has(self, k):
        return not isinstance(self.b, int) or 0 <= self.b + k < B

    def ring(self, k):
        return (self.parity + k) % 2


def turns(eng, iteration):
    for b in range(-2, 2):
        iteration(Turn(b // 2, b % 2))
    with eng.Fori(0, B // 2 - 2) as i:
        iteration(Turn(Count(i, 1, 1), 0))
        iteration(Turn(Count(i, 1, 1), 1))
    for b in range(B - 2, B + 2):
        iteration(Turn(b // 2, b % 2))


def after(eng, sem, count):
    if not isinstance(count, int) or count > 0:
        eng.wait_ge(sem, at(count))


def decoder_kernel(nc, x, ctx_kv, ln_gamma, ln_beta, w_qkv, w_out, b_out, gate_w, gate_b,
                   w1, b1, w2, b2, ffn_g, ffn_b, rope, masks, out):
    with ExitStack() as stack:
        def sb(name, shape, dt=F32):
            return stack.enter_context(nc.sbuf_tensor(name, shape, dt))

        def sem(name):
            return stack.enter_context(nc.semaphore(name))

        gates_dram = nc.dram_tensor("gates_by_expert", (E, B * N), F32, kind="Internal").ap()

        ps = stack.enter_context(nc.psum_tensor("ps", [128, 8, 512], F32))
        proj_ps = [ps[:, 0, :], ps[:, 1, :]]
        turn_ps = ps[:, 2, :]
        score_ps = [ps[:, 3, :], ps[:, 4, :]]
        probsT_ps = ps[:, 5, :]
        pv_ps = ps[:, 6, :]
        small_ps = ps[:, 7, 0:N]
        h_ps = [ps[:, n, :] for n in range(4)]
        oe_ps = [ps[:, 4, :], ps[:, 5, :]]
        b2_ps = ps[:, 6, :]
        fin_ps = ps[:, 7, :]

        ident = sb("ident", [128, 128])
        cmask = sb("cmask", [128, 128])
        iota8 = sb("iota8", [128, E])
        ropes = sb("ropes", [128, 2, 2, HD])
        vec_rows = sb("vec_rows", [2 + E * FT, 128])
        vec_cols = sb("vec_cols", [128, 2 + E * FT])
        gamma, beta = vec_cols[:, 0:1], vec_cols[:, 1:2]
        bout_bc = sb("bout_bc", [128, D])
        gateb_bc = sb("gateb_bc", [128, E])
        ffng_bc = sb("ffng_bc", [128, D])
        ffnb_bc = sb("ffnb_bc", [128, D])
        gatew = sb("gatew", [128, E])
        b2_rows = sb("b2_rows", [E, D])
        half = sb("half", [128, 1])
        hold = sb("hold", [128, 1])
        wqkv_in = sb("wqkv_in", [128, 2, CHUNK])
        wqkv_hi = sb("wqkv_hi", [128, 6, CHUNK], F32R)
        wqkv_lo = sb("wqkv_lo", [128, 6, CHUNK], F32R)
        wout = sb("wout", [128, PAIRS, D])
        w_stage = sb("w_stage", [128, 2, 2, WCOLS])
        w_hi = sb("w_hi", [128, 2, E * F], F32R)
        w_lo = sb("w_lo", [128, 2, E * F], F32R)

        x_all = sb("x_all", [128, B, D])
        ctx_in = sb("ctx_in", [128, 2, D])
        xc = sb("xc", [128, 2, D])
        xn_f = sb("xn_f", [128, 2, N])
        xn_hi = sb("xn_hi", [128, 2, N], F32R)
        xn_lo = sb("xn_lo", [128, 2, N], F32R)
        rope_cos = sb("rope_cos", [128, 2, CHUNK])
        rope_sin = sb("rope_sin", [128, 2, CHUNK])
        rot = sb("rot", [128, 2, CHUNK])
        rotT = sb("rotT", [128, 2, 2, PAIRS, N])
        v_sb = sb("v_sb", [128, 2, H * HD])
        probs = sb("probs", [128, QUADS, 4, N])
        negmax = sb("negmax", [128, QUADS, 4])
        den = sb("den", [128, QUADS, 4])
        rden = sb("rden", [128, QUADS, 4])
        probsT = sb("probsT", [128, 2, 4, N])
        headsT = sb("headsT", [128, 2, PAIRS, N])
        y1 = sb("y1", [128, D])
        x1 = sb("x1", [128, 2, D])
        x1ctxT = sb("x1ctxT", [128, 2, N])
        cdots = sb("cdots", [128, N])
        cprobs = sb("cprobs", [128, N])
        cprobsT = sb("cprobsT", [128, N])
        cneg = sb("cneg", [128, 2])
        cden = sb("cden", [128, 2])
        y2 = sb("y2", [128, D])
        x2 = sb("x2", [128, 2, D])
        x2T = sb("x2T", [128, B * N])
        x2T_hi = sb("x2T_hi", [128, B * N], F32R)
        x2T_lo = sb("x2T_lo", [128, B * N], F32R)

        g_f = [rope_cos[:, n, :] for n in range(2)]
        g_hi = wqkv_hi[:, 0:4, :]
        g_lo = wqkv_lo[:, 0:4, :]
        gates_bc = rotT[:, :, :, :, :].rearrange("p r q a b -> p (r q a b)").rearrange("p (e n) -> p e n", e=E)
        weighted = [probs[:, n, :, :].rearrange("p a b -> p (a b)") for n in range(2)]
        acc = probs[:, 2, :, :].rearrange("p a b -> p (a b)")
        logits = sb("logits", [128, B, E])
        top = sb("top", [128, B, 8])
        top_at = sb("top_at", [128, B, 8], U32)
        top_atf = sb("top_atf", [128, B, 2])
        pair_g = sb("pair_g", [128, 4, B])
        hot = sb("hot", [128, 2, B, E])
        gates = sb("gates", [128, B, E])
        gatesT = headsT[0:E, :, :, :].rearrange("p r a b -> p (r a b)")
        z1 = v_sb[:, 0, 0:BLOCK].rearrange("p (t d) -> p t d", t=TPB)
        z2 = v_sb[:, 0, BLOCK:2 * BLOCK].rearrange("p (t d) -> p t d", t=TPB)
        res = v_sb[:, 1, 0:BLOCK].rearrange("p (t d) -> p t d", t=TPB)

        class Norm:

            def __init__(self, name, tiles=1):
                self.stats = sb(name + "_stats", [128, tiles, 6])
                self.mv = sb(name + "_mv", [128, tiles, 2])
                self.veps = sb(name + "_veps", [128, tiles])
                self.rstd = sb(name + "_rstd", [128, tiles])
                self.s_stats = sem(name + "_stats_made")
                self.s_mv = sem(name + "_moments_made")
                self.s_veps = sem(name + "_veps_made")
                self.s_rstd = sem(name + "_rstd_made")

            def moments(self, dve, tiles, n):
                k = len(tiles)
                for t, tile in enumerate(tiles):
                    dve.bn_stats(self.stats[:, t, :], tile).then_inc(self.s_stats, 1)
                dve.wait_ge(self.s_stats, at(k * n))
                dve.memset(hold[:, :], 0.0)
                for t in range(k):
                    dve.bn_aggr(self.mv[:, t, :], self.stats[:, t, :]).then_inc(self.s_mv, 1)
                dve.wait_ge(self.s_mv, at(k * n))
                dve.tensor_scalar(self.veps[:, 0:k], self.mv[:, :, 1], EPS, None,
                                  ALU.add).then_inc(self.s_veps, 1)

            def root(self, pool, n):
                pool.wait_ge(self.s_veps, at(n))
                k = self.rstd.shape[1]
                pool.tensor_tensor(self.rstd[:, :], self.veps[:, :], half[:, :].to_broadcast([128, k]),
                                   ALU.pow).then_inc(self.s_rstd, 1)

        norm_x, norm_1, norm_2 = Norm("norm_x"), Norm("norm_1"), Norm("norm_2")
        norm_f, norm_3 = Norm("norm_f", TPB), Norm("norm_3", TPB)

        s_x = [sem("x_first_loaded"), sem("x_rest_loaded")]
        s_const = sem("consts_loaded")
        s_wqkv = [sem("wqkv_even_loaded"), sem("wqkv_odd_loaded")]
        s_ctx = [sem("ctx_even_loaded"), sem("ctx_odd_loaded")]
        s_w = [sem("w_even_loaded"), sem("w_odd_loaded")]
        s_turned = sem("four_transposed")
        s_proj = sem("proj_made")
        s_rotT = sem("rot_transposed")
        s_scores = sem("scores_made")
        s_probsT = sem("probs_transposed")
        s_pv = sem("pv_made")
        s_attn = sem("attn_out_made")
        s_dots = sem("cross_dots_made")
        s_cprobsT = sem("cross_probs_transposed")
        s_cross = sem("cross_out_made")
        s_vecT = sem("vec_transposed")
        s_vec = sem("vec_cols_made")
        s_half = sem("half_set")
        s_wqkv_lo = sem("wqkv_lo_made")
        s_xc = sem("xc_made")
        s_roped = sem("rope_products_made")
        s_negmax = sem("negmax_made")
        s_rden = sem("rden_made")
        s_heads = sem("heads_copied")
        s_y1 = sem("y1_made")
        s_x1 = sem("x1_made")
        s_cdots = sem("cross_dots_masked")
        s_cmax = sem("cross_max_made")
        s_cneg = sem("cross_negmax_made")
        s_crden = sem("cross_rden_made")
        s_y2 = sem("y2_made")
        s_x2 = sem("x2_made")
        s_wqkv_hi = sem("wqkv_hi_made")
        s_xn = sem("xn_made")
        s_rotT_sb = sem("rotT_copied")
        s_v = sem("v_copied")
        s_exp = sem("exp_made")
        s_probsT_sb = sem("probsT_copied")
        s_x1ctxT_sb = sem("x1ctxT_copied")
        s_cexp = sem("cross_exp_made")
        s_cprobsT_sb = sem("cross_probsT_copied")
        s_x2T_sb = sem("x2T_copied")
        s_w_hi = sem("w_hi_made")
        s_rot = sem("rot_made")
        s_probs = sem("probs_normalised")
        s_biased = sem("x_biased")
        s_xn_lo = sem("xn_lo_made")
        s_x2_kept = sem("x2_kept")
        s_x2_lo = sem("x2_lo_made")
        s_w_lo = sem("w_lo_made")
        s_logits = sem("logits_made")
        s_gsteps = sem("gating_steps_done")
        s_gexp = sem("gate_exp_made")
        s_gatesT = sem("gates_transposed")
        s_gatesT_sb = sem("gatesT_copied")
        s_gates_out = sem("gates_stored")
        s_gbc = [sem(f"gates_bc_loaded_{e}") for e in range(E)]
        s_h = sem("hidden_made")
        s_gelu = sem("gelu_made")
        s_g_lo = sem("gelu_lo_made")
        s_oe = sem("expert_out_made")
        s_b2 = sem("b2_part_made")
        s_weighted = sem("expert_weighted")
        s_acc = sem("experts_summed")
        s_fin = sem("moe_transposed")
        s_z = sem("ffn_normalised")
        s_affine = sem("ffn_affine_made")
        s_res = sem("final_normalised")
        s_out = sem("out_stored")

        block = stack.enter_context(nc.Block())

        def bcast(v):
            return v.rearrange("(a n) -> a n", a=1).to_broadcast([128, v.shape[0]])

        def store(sp, k):
            sp.wait_ge(s_res, at(k + 1))
            sp.dma_start(out[bass.ds(at(TPB * k), TPB)].rearrange("b p d -> p b d"), res).then_inc(s_out, 16)

        @block.sync
        def _(sp):
            sp.sem_inc(s_out, 16)
            x_t = x.rearrange("b p d -> p b d")
            sp.dma_start(x_all[:, 0:2, :], x_t[:, 0:2, :]).then_inc(s_x[0], 16)
            for c, col in enumerate(CHUNKS):
                if c >= 2:
                    sp.wait_ge(s_wqkv_lo, c - 1)
                sp.dma_start(wqkv_in[:, c % 2, :], w_qkv[:, col:col + CHUNK]).then_inc(s_wqkv[c % 2], 16)
                if c == 1:
                    sp.dma_start(x_all[:, 2:B, :], x_t[:, 2:B, :]).then_inc(s_x[1], 16)

            def iteration(t):
                if t.has(0):
                    r, b = t.ring(0), t.b
                    after(sp, s_cross, b - 1)
                    sp.dma_start(ctx_in[:, r, :], ctx_kv[at(t.b)]).then_inc(s_ctx[r], 16)
                    after(sp, s_w_lo, b - 1)
                    sp.dma_start(w_stage[:, r, 0, :],
                                 w1[at(t.i), :, r * WCOLS:(r + 1) * WCOLS]).then_inc(s_w[r], 16)
                    sp.dma_start(w_stage[:, r, 1, :].rearrange("p (f d) -> p f d", d=D),
                                 w2[at(t.i), r * 2 * 128:(r + 1) * 2 * 128, :].rearrange("(f p) d -> p f d", p=128)
                                 ).then_inc(s_w[r], 16)

            turns(sp, iteration)

            sp.wait_ge(s_gatesT_sb, TPB)
            sp.dma_start(gates_dram, gatesT[:, :]).then_inc(s_gates_out, 16)
            sp.wait_ge(s_gates_out, 16)

            def gates_of(k):
                for e in range(E):
                    after(sp, s_weighted, E * (k - 1) + e + 1)
                    sp.dma_start(gates_bc[:, e, :],
                                 gates_dram[e:e + 1, bass.ds(at(BLOCK * k), BLOCK)].to_broadcast([128, BLOCK])
                                 ).then_inc(s_gbc[e], 16)

            gates_of(0)
            with sp.Fori(0, NBLOCKS - 1) as k:
                gates_of(Count(k, 1, 1))
                store(sp, Count(k))
            store(sp, NBLOCKS - 1)
            sp.wait_ge(s_out, 16 * (NBLOCKS + 1))

        @block.scalar
        def _(act):
            smalls = [(ident[:, :], masks[0]), (ropes[:, :, :, :], rope), (vec_rows[0:1, :], ln_gamma.rearrange("(a n) -> a n", a=1)),
                      (vec_rows[1:2, :], ln_beta.rearrange("(a n) -> a n", a=1)), (bout_bc[:, :], bcast(b_out)),
                      (cmask[:, :], masks[1]), (iota8[:, :], masks[2][:, 0:E]), (gateb_bc[:, :], bcast(gate_b)),
                      (ffng_bc[:, :], bcast(ffn_g)), (ffnb_bc[:, :], bcast(ffn_b)), (gatew[:, :], gate_w),
                      (vec_rows[2:2 + E * FT, :], b1.rearrange("e (f p) -> (e f) p", p=128)), (b2_rows[:, :], b2),
                      (wout[:, :, :], w_out.rearrange("(t p) d -> p t d", p=128))]
            act.sem_inc(s_x2T_sb, X2T_CREDIT)
            for dst, src in smalls:
                act.dma_start(dst, src).then_inc(s_const, 16)
            for c in range(6):
                act.wait_ge(s_wqkv[c % 2], 16 * (c // 2 + 1))
                act.activation(wqkv_hi[:, c, :], wqkv_in[:, c % 2, :], ACT.Copy).then_inc(s_wqkv_hi, 1)
            act.wait_ge(s_const, CONSTS)
            act.wait_ge(s_vec, 1)

            def exps(b, t):
                act.wait_ge(s_negmax, at(4 * b + t + 1))
                after(act, s_probsT, 4 * (b - 1) + t + 1)
                for h in range(4):
                    e = act.activation(probs[:, t, h, :], score_ps[t % 2][:, h * N:(h + 1) * N], ACT.Exp,
                                       bias=negmax[:, t, h:h + 1], accum_out=den[:, t, h:h + 1])
                e.then_inc(s_exp, 1)

            def probsT_copy(b, t):
                act.wait_ge(s_probsT, at(4 * b + t + 1))
                after(act, s_pv, 2 * b + t // 2)
                act.activation(probsT[:, t % 2, :, :].rearrange("p a b -> p (a b)"), probsT_ps,
                               ACT.Copy).then_inc(s_probsT_sb, 1)

            def rotT_copy(b, r, c):
                act.wait_ge(s_rotT, at(4 * b + c + 1))
                act.activation(rotT[:, r, c % 2, 4 * (c // 2):4 * (c // 2) + 4, :],
                               turn_ps.rearrange("p (a b) -> p a b", a=4), ACT.Copy).then_inc(s_rotT_sb, 1)

            def iteration(t):
                b = t.b
                if t.has(0):
                    rotT_copy(b, t.ring(0), 3)
                if t.has(-1):
                    probsT_copy(b - 1, 2)
                if t.has(0):
                    exps(b, 0)
                if t.has(-2):
                    act.wait_ge(s_cneg, at(b - 2 + 1))
                    act.activation(cprobs[:, :], cdots[:, :], ACT.Exp, bias=cneg[:, 1:2], scale=CROSS_SCALE,
                                   accum_out=cden[:, 0:1]).then_inc(s_cexp, 1)
                if t.has(-1):
                    probsT_copy(b - 1, 3)
                if t.has(0):
                    exps(b, 1)
                if t.has(-2):
                    act.wait_ge(s_cprobsT, at(b - 2 + 1))
                    act.activation(cprobsT[:, :], turn_ps[:, 0:N], ACT.Copy).then_inc(s_cprobsT_sb, 1)
                if t.has(1):
                    rotT_copy(b + 1, t.ring(1), 0)
                if t.has(0):
                    probsT_copy(b, 0)
                    exps(b, 2)
                if t.has(1):
                    rotT_copy(b + 1, t.ring(1), 1)
                if t.has(0):
                    act.wait_ge(s_w[t.ring(0)], at(32 * (t.i + 1)))
                    act.activation(w_hi[:, :, bass.ds(at(b * WCOLS), WCOLS)], w_stage[:, t.ring(0), :, :],
                                   ACT.Copy).then_inc(s_w_hi, 1)
                if t.has(0):
                    probsT_copy(b, 1)
                    exps(b, 3)
                if t.has(1):
                    after(act, s_pv, 2 * b)
                    for j in range(2):
                        act.wait_ge(s_proj, at(6 * (b + 1) + 5 + j))
                        act.activation(v_sb[:, t.ring(1), j * CHUNK:(j + 1) * CHUNK], proj_ps[j],
                                       ACT.Copy).then_inc(s_v, 1)
                    rotT_copy(b + 1, t.ring(1), 2)
                act.wait_ge(s_turned, at(b + 3))
                if t.has(-1):
                    act.activation(x1ctxT[:, :, :].rearrange("p a b -> p (a b)"), turn_ps[:, 0:2 * N],
                                   ACT.Copy).then_inc(s_x1ctxT_sb, 1)
                if t.has(2):
                    after(act, s_proj, 6 * (b + 1))
                    for xn in (xn_f, xn_hi):
                        act.activation(xn[:, t.ring(2), :], turn_ps[:, 3 * N:4 * N], ACT.Identity, bias=beta,
                                       scale=gamma).then_inc(s_xn, 1)
                if t.has(-2):
                    for x2_turned in (x2T, x2T_hi):
                        act.activation(x2_turned[:, bass.ds(at((b - 2) * N), N)], turn_ps[:, 2 * N:3 * N],
                                       ACT.Copy).then_inc(s_x2T_sb, 1)

            turns(act, iteration)

            act.wait_ge(s_gsteps, GATE_DIFF)
            act.activation(pair_g[:, 1, :], pair_g[:, 0, :], ACT.Exp).then_inc(s_gexp, 1)

            def block_of(k):
                for s in range(E * FT):
                    act.wait_ge(s_h, at(E * FT * k + s + 1))
                    after(act, s_g_lo, E * FT * k + s - 1)
                    after(act, s_oe, E * FT * k + s - 3)
                    b1_col = vec_cols[:, 2 + s:3 + s]
                    act.activation(g_f[s % 2], h_ps[s % 4], ACT.Gelu, bias=b1_col).then_inc(s_gelu, 1)
                    act.activation(g_hi[:, s % 4, :], h_ps[s % 4], ACT.Gelu,
                                   bias=b1_col).then_inc(s_gelu, 1)

            block_of(0)
            with act.Fori(0, NBLOCKS - 1) as k:
                block_of(Count(k, 1, 1))

        @block.gpsimd
        def _(pool):
            pool.wait_ge(s_const, CONSTS)
            pool.wait_ge(s_half, 1)

            def rotate(b, c):
                pool.wait_ge(s_roped, at(4 * b + c + 1))
                after(pool, s_rotT, 4 * b + c - 1)
                o = rot[:, c % 2, :].rearrange("p (h s j) -> p h s j", s=2, j=HD // 2)
                co = rope_cos[:, c % 2, :].rearrange("p (h s j) -> p h s j", s=2, j=HD // 2)
                si = rope_sin[:, c % 2, :].rearrange("p (h s j) -> p h s j", s=2, j=HD // 2)
                pool.tensor_tensor(o[:, :, 0, :], co[:, :, 0, :], si[:, :, 1, :], ALU.add)
                pool.tensor_tensor(o[:, :, 1, :], co[:, :, 1, :], si[:, :, 0, :], ALU.add).then_inc(s_rot, 1)

            def normalise(b, t):
                pool.wait_ge(s_rden, at(4 * b + t + 1))
                pool.tensor_tensor(probs[:, t, :, :], probs[:, t, :, :],
                                   rden[:, t, :].unsqueeze(2).to_broadcast([128, 4, N]),
                                   ALU.mult).then_inc(s_probs, 1)

            def iteration(t):
                b = t.b
                if t.has(-1):
                    normalise(b - 1, 3)
                if t.has(1):
                    rotate(b + 1, 0)
                    rotate(b + 1, 1)
                if t.has(0):
                    normalise(b, 0)
                if t.has(2):
                    norm_x.root(pool, b + 2 + 1)
                if t.has(1):
                    rotate(b + 1, 2)
                if t.has(0):
                    normalise(b, 1)
                if t.has(-1):
                    norm_1.root(pool, b)
                if t.has(-2):
                    norm_2.root(pool, b - 1)
                if t.has(1):
                    rotate(b + 1, 3)
                if t.has(0):
                    normalise(b, 2)
                if t.has(2):
                    pool.wait_ge(s_xc, at(b + 2 + 1))
                    pool.tensor_tensor(x_all[:, bass.ds(at(b + 2), 1), :], x_all[:, bass.ds(at(b + 2), 1), :],
                                       bout_bc[:, :].unsqueeze(1), ALU.add).then_inc(s_biased, 1)
                    pool.wait_ge(s_xn, at(2 * (b + 2) + 2))
                    pool.tensor_tensor(xn_lo[:, t.ring(2), :], xn_f[:, t.ring(2), :], xn_hi[:, t.ring(2), :],
                                       ALU.subtract).then_inc(s_xn_lo, 1)
                if t.has(-2):
                    pool.wait_ge(s_x2, at(b - 2 + 1))
                    pool.tensor_copy(x_all[:, bass.ds(at(b - 2), 1), :], x2[:, t.ring(0), :].unsqueeze(1)).then_inc(s_x2_kept, 1)
                    pool.wait_ge(s_x2T_sb, at(2 * (b - 2) + 2 + X2T_CREDIT))
                    pool.tensor_tensor(x2T_lo[:, bass.ds(at((b - 2) * N), N)], x2T[:, bass.ds(at((b - 2) * N), N)],
                                       x2T_hi[:, bass.ds(at((b - 2) * N), N)], ALU.subtract).then_inc(s_x2_lo, 1)
                if t.has(0):
                    pool.wait_ge(s_w_hi, at(b + 1))
                    pool.tensor_tensor(w_lo[:, :, bass.ds(at(b * WCOLS), WCOLS)], w_stage[:, t.ring(0), :, :],
                                       w_hi[:, :, bass.ds(at(b * WCOLS), WCOLS)], ALU.subtract).then_inc(s_w_lo, 1)

            turns(pool, iteration)

            def sum_expert(k, e):
                pool.wait_ge(s_weighted, at(E * k + e + 1))
                pool.wait_ge(s_acc, at(E * k + e))
                pool.tensor_tensor(acc, acc, weighted[e % 2], ALU.add).then_inc(s_acc, 1)

            def finish(k):
                norm_f.root(pool, k + 1)
                pool.wait_ge(s_z, at(4 * k + 4))
                pool.tensor_tensor(z2, z1, ffng_bc[:, :].unsqueeze(1).to_broadcast([128, TPB, D]),
                                   ALU.mult).then_inc(s_affine, 1)
                pool.wait_ge(s_affine, at(3 * k + 1))
                pool.tensor_tensor(z2, z2, ffnb_bc[:, :].unsqueeze(1).to_broadcast([128, TPB, D]),
                                   ALU.add).then_inc(s_affine, 1)
                pool.wait_ge(s_affine, at(3 * k + 2))
                pool.tensor_tensor(z2, z2, x_all[:, bass.ds(at(TPB * k), TPB), :], ALU.add).then_inc(s_affine, 1)
                norm_3.root(pool, k + 1)

            def block_of(k, first):
                for e in range(1, E):
                    if e == 2 and not first:
                        finish(k - 1)
                    sum_expert(k, e)

            block_of(0, True)
            with pool.Fori(0, NBLOCKS - 1) as k:
                block_of(Count(k, 1, 1), False)
            finish(NBLOCKS - 1)

        @block.vector
        def _(dve):
            dve.memset(half[:, :], -0.5).then_inc(s_half, 1)

            def rope_products(b, c):
                dve.wait_ge(s_proj, at(6 * b + c + 1))
                after(dve, s_rot, 4 * b + c - 1)
                p = proj_ps[c % 2].rearrange("p (h j) -> p h j", j=HD)
                for kind, dst in ((COS, rope_cos), (SIN, rope_sin)):
                    table = ropes[:, c % 2, kind, :].unsqueeze(1).to_broadcast([128, CHUNK // HD, HD])
                    ins = dve.tensor_tensor(dst[:, c % 2, :].rearrange("p (h j) -> p h j", j=HD), p, table, ALU.mult)
                ins.then_inc(s_roped, 1)

            def row_max(b, t):
                dve.wait_ge(s_scores, at(4 * b + t + 1))
                dve.tensor_reduce(negmax[:, t, :], score_ps[t % 2].rearrange("p (h k) -> p h k", h=4), AX.X,
                                  ALU.max, negate=True).then_inc(s_negmax, 1)

            def recip(b, t):
                dve.wait_ge(s_exp, at(4 * b + t + 1))
                dve.reciprocal(rden[:, t, :], den[:, t, :]).then_inc(s_rden, 1)

            def heads_copy(b, r, o):
                dve.wait_ge(s_pv, at(2 * b + o + 1))
                dve.tensor_copy(headsT[:, r, 4 * o:4 * o + 4, :].rearrange("p a b -> p (a b)"),
                                pv_ps).then_inc(s_heads, 1)

            def normed(norm, n, dst, src):
                dve.wait_ge(norm.s_rstd, at(n))
                return dve.tensor_scalar(dst, src, norm.mv[:, 0, 0:1], norm.rstd[:, 0:1], ALU.subtract, ALU.mult)

            def split_wqkv(c):
                dve.wait_ge(s_wqkv_hi, c + 1)
                dve.tensor_tensor(wqkv_lo[:, c, :], wqkv_in[:, c % 2, :], wqkv_hi[:, c, :],
                                  ALU.subtract).then_inc(s_wqkv_lo, 1)

            def iteration(t):
                b = t.b
                if t.has(0):
                    row_max(b, 0)
                if t.has(-1):
                    heads_copy(b - 1, t.ring(-1), 0)
                if t.has(1):
                    rope_products(b + 1, 0)
                if t.has(-2):
                    dve.wait_ge(s_dots, at(b - 1))
                    dve.tensor_tensor(cdots[:, :], small_ps, cmask[:, :], ALU.add).then_inc(s_cdots, 1)
                    dve.wait_ge(s_cdots, at(b - 1))
                    dve.tensor_reduce(cneg[:, 0:1], cdots[:, :], AX.X, ALU.max, negate=True).then_inc(s_cmax, 1)
                    dve.wait_ge(s_cmax, at(b - 1))
                    dve.tensor_scalar(cneg[:, 1:2], cneg[:, 0:1], CROSS_SCALE, None, ALU.mult).then_inc(s_cneg, 1)
                if t.has(0):
                    recip(b, 0)
                if t.has(1):
                    rope_products(b + 1, 1)
                if t.has(0):
                    row_max(b, 1)
                if t.has(-2):
                    dve.wait_ge(s_cexp, at(b - 1))
                    dve.reciprocal(cden[:, 1:2], cden[:, 0:1]).then_inc(s_crden, 1)
                if t.has(2):
                    if isinstance(b, int):
                        dve.wait_ge(s_x[0 if b + 2 < 2 else 1], 16)
                    norm_x.moments(dve, [x_all[:, bass.ds(at(b + 2), 1), :].rearrange("p a d -> p (a d)")], b + 2 + 1)
                if t.has(1):
                    rope_products(b + 1, 2)
                if t.has(0):
                    recip(b, 1)
                if t.has(-1):
                    heads_copy(b - 1, t.ring(-1), 1)
                if t.has(2):
                    after(dve, s_turned, b + 1)
                    normed(norm_x, b + 2 + 1, xc[:, t.ring(2), :],
                           x_all[:, bass.ds(at(b + 2), 1), :].rearrange("p a d -> p (a d)")).then_inc(s_xc, 1)
                if t.has(0):
                    row_max(b, 2)
                if t.has(-1):
                    dve.wait_ge(s_attn, at(b))
                    dve.wait_ge(s_biased, at(b))
                    dve.tensor_tensor(y1[:, :], small_ps, x_all[:, bass.ds(at(b - 1), 1), :].rearrange("p a d -> p (a d)"),
                                      ALU.add).then_inc(s_y1, 1)
                    dve.wait_ge(s_y1, at(b))
                    norm_1.moments(dve, [y1[:, :]], b)
                if t.has(-2):
                    dve.wait_ge(s_cross, at(b - 1))
                    dve.wait_ge(s_crden, at(b - 1))
                    dve.scalar_tensor_tensor(y2[:, :], small_ps, cden[:, 1:2], x1[:, t.ring(0), :], ALU.mult,
                                             ALU.add).then_inc(s_y2, 1)
                    dve.wait_ge(s_y2, at(b - 1))
                    norm_2.moments(dve, [y2[:, :]], b - 1)
                if t.has(1):
                    rope_products(b + 1, 3)
                if t.has(0):
                    recip(b, 2)
                if t.has(-1):
                    normed(norm_1, b, x1[:, t.ring(-1), :], y1[:, :]).then_inc(s_x1, 1)
                if t.has(-2):
                    normed(norm_2, b - 1, x2[:, t.ring(0), :], y2[:, :]).then_inc(s_x2, 1)
                if t.has(0):
                    row_max(b, 3)
                    recip(b, 3)
                if isinstance(b, int) and b == -2:
                    for c in range(6):
                        split_wqkv(c)

            dve.wait_ge(s_const, CONSTS)
            dve.wait_ge(s_vecT, 1)
            dve.tensor_copy(vec_cols[:, :], probsT_ps[:, 0:2 + E * FT]).then_inc(s_vec, 1)
            turns(dve, iteration)

            steps = [0]

            def step(ins):
                ins.then_inc(s_gsteps, 1)
                steps[0] += 1
                dve.wait_ge(s_gsteps, steps[0])

            dve.wait_ge(s_logits, 1)
            step(dve.tensor_tensor(logits[:, :, :], b2_ps[:, 0:B * E].rearrange("p (t e) -> p t e", e=E),
                                   gateb_bc[:, :].unsqueeze(1).to_broadcast([128, B, E]), ALU.add))
            step(dve.tensor_scalar(logits[:, :, :], logits[:, :, :], INV_TEMP, None, ALU.mult))
            for n in range(B):
                ins = dve.max(top[:, n, :], logits[:, n, :])
            step(ins)
            step(dve.tensor_tensor(pair_g[:, 0, :], top[:, :, 1], top[:, :, 0], ALU.subtract))
            assert steps[0] == GATE_DIFF
            for n in range(B):
                ins = dve.max_index(top_at[:, n, :], top[:, n, :], logits[:, n, :])
            step(ins)
            step(dve.tensor_copy(top_atf[:, :, :], top_at[:, :, 0:2]))
            for j in range(2):
                ins = dve.tensor_tensor(hot[:, j, :, :], iota8[:, :].unsqueeze(1).to_broadcast([128, B, E]),
                                        top_atf[:, :, j:j + 1].to_broadcast([128, B, E]), ALU.is_equal)
            step(ins)
            dve.wait_ge(s_gexp, 1)
            step(dve.tensor_scalar(pair_g[:, 0, :], pair_g[:, 1, :], 1.0, None, ALU.add))
            step(dve.reciprocal(pair_g[:, 2, :], pair_g[:, 0, :]))
            step(dve.tensor_tensor(pair_g[:, 3, :], pair_g[:, 1, :], pair_g[:, 2, :], ALU.mult))
            for j in range(2):
                ins = dve.tensor_tensor(hot[:, j, :, :], hot[:, j, :, :],
                                        pair_g[:, 2 + j, :].unsqueeze(2).to_broadcast([128, B, E]), ALU.mult)
            step(ins)
            step(dve.tensor_tensor(gates[:, :, :], hot[:, 0, :, :], hot[:, 1, :, :], ALU.add))
            assert steps[0] == GATES_MADE

            def gates_copy(k):
                dve.wait_ge(s_gatesT, at(k + 1))
                dve.tensor_copy(gatesT[:, k * BLOCK:(k + 1) * BLOCK],
                                (b2_ps, fin_ps)[k % 2][0:E, :]).then_inc(s_gatesT_sb, 1)

            def weigh(k, e):
                dve.wait_ge(s_oe, at(E * FT * k + FT * (e + 1)))
                dve.wait_ge(s_gbc[e], at(16 * (k + 1)))
                after(dve, s_acc, E * k + e - 1)
                dve.tensor_tensor(weighted[e % 2], oe_ps[e % 2], gates_bc[:, e, :], ALU.mult).then_inc(s_weighted, 1)
                if e == 0:
                    dve.wait_ge(s_weighted, at(E * k + 1))
                    dve.wait_ge(s_b2, at(k + 1))
                    after(dve, s_fin, k)
                    dve.tensor_tensor(acc, weighted[0], b2_ps, ALU.add).then_inc(s_acc, 1)

            def finish_stats(k):
                dve.wait_ge(s_fin, at(k + 1))
                norm_f.moments(dve, [fin_ps[:, n * N:(n + 1) * N] for n in range(TPB)], k + 1)

            def finish_norm(k):
                dve.wait_ge(norm_f.s_rstd, at(k + 1))
                for n in range(TPB):
                    dve.tensor_scalar(z1[:, n, :], fin_ps[:, n * N:(n + 1) * N], norm_f.mv[:, n, 0:1],
                                      norm_f.rstd[:, n:n + 1], ALU.subtract, ALU.mult).then_inc(s_z, 1)

            def finish_stats2(k):
                dve.wait_ge(s_affine, at(3 * k + 3))
                norm_3.moments(dve, [z2[:, n, :] for n in range(TPB)], k + 1)

            def finish_norm2(k):
                dve.wait_ge(norm_3.s_rstd, at(k + 1))
                dve.wait_ge(s_out, at(16 * (k + 1)))
                for n in range(TPB):
                    ins = dve.tensor_scalar(res[:, n, :], z2[:, n, :], norm_3.mv[:, n, 0:1],
                                            norm_3.rstd[:, n:n + 1], ALU.subtract, ALU.mult)
                ins.then_inc(s_res, 1)

            def block_of(k, first):
                for s in range(E * FT):
                    dve.wait_ge(s_gelu, at(2 * (E * FT * k + s) + 2))
                    after(dve, s_oe, E * FT * k + s - 3)
                    dve.tensor_tensor(g_lo[:, s % 4, :], g_f[s % 2], g_hi[:, s % 4, :],
                                      ALU.subtract).then_inc(s_g_lo, 1)
                    if first and s < TPB:
                        gates_copy(s)
                    if s % FT == 2 and s > FT:
                        weigh(k, s // FT - 1)
                    if not first:
                        if s == 2:
                            weigh(k - 1, E - 1)
                        if s == 9:
                            finish_stats(k - 1)
                        if s == 12:
                            finish_norm(k - 1)
                        if s == 17:
                            finish_stats2(k - 1)
                        if s == 20:
                            finish_norm2(k - 1)

            block_of(0, True)
            with dve.Fori(0, NBLOCKS - 1) as k:
                block_of(Count(k, 1, 1), False)
            k = NBLOCKS - 1
            weigh(k, E - 1)
            finish_stats(k)
            finish_norm(k)
            finish_stats2(k)
            finish_norm2(k)

        @block.tensor
        def _(pe):
            pe.wait_ge(s_const, CONSTS)
            pe.transpose(probsT_ps[:, 0:2 + E * FT], vec_rows[:, :], ident[0:2 + E * FT, 0:2 + E * FT]).then_inc(s_vecT, 1)

            def project(b, r, c):
                if c == 0:
                    pe.wait_ge(s_xn_lo, at(b + 1))
                if c < 2:
                    after(pe, s_v, 2 * b + c - 1)
                else:
                    pe.wait_ge(s_roped, at(4 * b + c - 1))
                if isinstance(b, int) and b == 0:
                    pe.wait_ge(s_wqkv_lo, c + 1)
                pe.matmul(proj_ps[c % 2], xn_hi[:, r, :], wqkv_hi[:, c, :], start=True, stop=False)
                pe.matmul(proj_ps[c % 2], xn_hi[:, r, :], wqkv_lo[:, c, :], start=False, stop=False)
                pe.matmul(proj_ps[c % 2], xn_lo[:, r, :], wqkv_hi[:, c, :], start=False,
                          stop=True).then_inc(s_proj, 1)

            def turned_copied(b):
                after(pe, s_x1ctxT_sb, made(b, B))
                after(pe, s_xn, made(2 * (b + 3), 2 * B))
                after(pe, s_x2T_sb, 2 * (b - 1) + X2T_CREDIT)

            def transpose_rot(b, c):
                pe.wait_ge(s_rot, at(4 * b + c + 1))
                after(pe, s_rotT_sb, 4 * b + c)
                if c == 0:
                    after(pe, s_cprobsT_sb, b - 2)
                if c == 3:
                    turned_copied(b - 1)
                for p in range(4):
                    ins = pe.transpose(turn_ps[:, p * N:(p + 1) * N], rot[:, c % 2, p * 128:(p + 1) * 128], ident[:, :])
                ins.then_inc(s_rotT, 1)

            def turn_four(t):
                b = t.b
                after(pe, s_rotT_sb, made(4 * (b + 1) + 3, 4 * B))
                after(pe, s_cprobsT_sb, b - 1)
                turned_copied(b - 1)
                if t.has(-1):
                    pe.wait_ge(s_x1, at(b))
                    pe.wait_ge(s_ctx[t.ring(-1)], at(16 * (t.i + t.parity)))
                    pe.transpose(turn_ps[:, 0:N], x1[:, t.ring(-1), :], ident[:, :])
                    ins = pe.transpose(turn_ps[:, N:2 * N], ctx_in[:, t.ring(-1), :], ident[:, :])
                if t.has(-2):
                    pe.wait_ge(s_x2, at(b - 1))
                    ins = pe.transpose(turn_ps[:, 2 * N:3 * N], x2[:, t.ring(0), :], ident[:, :])
                if t.has(2):
                    pe.wait_ge(s_xc, at(b + 3))
                    ins = pe.transpose(turn_ps[:, 3 * N:4 * N], xc[:, t.ring(2), :], ident[:, :])
                ins.then_inc(s_turned, 1)

            def scores(b, r, t):
                pe.wait_ge(s_rotT_sb, at(4 * b + (2 if t < 2 else 4)))
                after(pe, s_exp, 4 * b + t - 1)
                for j in range(4):
                    pair, side = head_of(t, j)
                    rows = slice(HD * side, HD * side + HD)
                    ins = pe.matmul(score_ps[t % 2][:, j * N:(j + 1) * N], rotT[rows, r, 0, pair, :],
                                    rotT[rows, r, 1, pair, :], start=True, stop=True)
                ins.then_inc(s_scores, 1)

            def transpose_probs(b, t):
                pe.wait_ge(s_probs, at(4 * b + t + 1))
                after(pe, s_probsT_sb, 4 * b + t)
                for j in range(4):
                    ins = pe.transpose(probsT_ps[:, j * N:(j + 1) * N], probs[:, t, j, :], ident[:, :])
                ins.then_inc(s_probsT, 1)

            def values(b, r, o):
                pe.wait_ge(s_probsT_sb, at(4 * b + 2 * o + 2))
                pe.wait_ge(s_v, at(2 * b + 2))
                after(pe, s_heads, 2 * b + o)
                for j in range(8):
                    quad = 2 * o + j % 2
                    pair, side = head_of(quad, j // 2)
                    h = 2 * pair + side
                    ins = pe.matmul(pv_ps[HD * side:HD * side + HD, (j // 2) * N:(j // 2 + 1) * N],
                                    v_sb[:, r, h * HD:(h + 1) * HD], probsT[:, quad % 2, j // 2, :],
                                    start=True, stop=True)
                ins.then_inc(s_pv, 1)

            def iteration(t):
                b = t.b
                if t.has(0):
                    scores(b, t.ring(0), 0)
                if t.has(-1):
                    values(b - 1, t.ring(-1), 0)
                    transpose_probs(b - 1, 2)
                if t.has(1):
                    project(b + 1, t.ring(1), 0)
                if t.has(-2):
                    pe.wait_ge(s_x1ctxT_sb, at(b - 1))
                    pe.matmul(small_ps, x1ctxT[:, 0, :], x1ctxT[:, 1, :], start=True, stop=True).then_inc(s_dots, 1)
                if t.has(1):
                    project(b + 1, t.ring(1), 1)
                if t.has(0):
                    transpose_rot(b, 3)
                    scores(b, t.ring(0), 1)
                if t.has(-1):
                    transpose_probs(b - 1, 3)
                if t.has(1):
                    project(b + 1, t.ring(1), 2)
                if t.has(-2):
                    pe.wait_ge(s_cexp, at(b - 1))
                    after(pe, s_rotT_sb, made(4 * (b + 1), 4 * B))
                    turned_copied(b - 1)
                    pe.transpose(turn_ps[:, 0:N], cprobs[:, :], ident[:, :]).then_inc(s_cprobsT, 1)
                if t.has(1):
                    transpose_rot(b + 1, 0)
                if t.has(-1):
                    values(b - 1, t.ring(-1), 1)
                if t.has(0):
                    scores(b, t.ring(0), 2)
                    transpose_probs(b, 0)
                if t.has(1):
                    project(b + 1, t.ring(1), 3)
                if t.has(-1):
                    pe.wait_ge(s_heads, at(2 * b))
                    after(pe, s_cdots, b - 1)
                    for p in range(PAIRS):
                        ins = pe.matmul(small_ps, headsT[:, t.ring(-1), p, :], wout[:, p, :], start=(p == 0),
                                        stop=(p == PAIRS - 1))
                    ins.then_inc(s_attn, 1)
                if t.has(1):
                    transpose_rot(b + 1, 1)
                if t.has(-2):
                    pe.wait_ge(s_cprobsT_sb, at(b - 1))
                    pe.wait_ge(s_y1, at(made(b, B)))
                    pe.matmul(small_ps, cprobsT[:, :], ctx_in[:, t.ring(0), :], start=True, stop=True).then_inc(s_cross, 1)
                if t.has(0):
                    scores(b, t.ring(0), 3)
                    transpose_probs(b, 1)
                if t.has(1):
                    project(b + 1, t.ring(1), 4)
                    project(b + 1, t.ring(1), 5)
                    transpose_rot(b + 1, 2)
                turn_four(t)

            turns(pe, iteration)

            pe.wait_ge(s_x2T_sb, 2 * B + X2T_CREDIT)
            for n in range(B):
                ins = pe.matmul(b2_ps[:, n * E:(n + 1) * E], x2T[:, n * N:(n + 1) * N], gatew[:, :], start=True, stop=True)
            ins.then_inc(s_logits, 1)
            pe.wait_ge(s_x2_lo, B)
            pe.wait_ge(s_w_lo, B)

            def hidden(k, s):
                e, f = s // FT, s % FT
                after(pe, s_gelu, 2 * (E * FT * k + s - 3))
                hi, lo = (w[:, 0, s * 128:(s + 1) * 128] for w in (w_hi, w_lo))
                x_hi, x_lo = (a[:, bass.ds(at(BLOCK * k), BLOCK)] for a in (x2T_hi, x2T_lo))
                pe.matmul(h_ps[s % 4], hi, x_hi, start=True, stop=False)
                pe.matmul(h_ps[s % 4], hi, x_lo, start=False, stop=False)
                pe.matmul(h_ps[s % 4], lo, x_hi, start=False, stop=True).then_inc(s_h, 1)

            def expert_out(k, s):
                e, f = s // FT, s % FT
                pe.wait_ge(s_g_lo, at(E * FT * k + s + 1))
                if f == 0:
                    after(pe, s_weighted, E * k + e - 1)
                hi, lo = (w[:, 1, s * 128:(s + 1) * 128] for w in (w_hi, w_lo))
                pe.matmul(oe_ps[e % 2], hi, g_hi[:, s % 4, :], start=(f == 0), stop=False)
                pe.matmul(oe_ps[e % 2], lo, g_hi[:, s % 4, :], start=False, stop=False)
                pe.matmul(oe_ps[e % 2], hi, g_lo[:, s % 4, :], start=False, stop=(f == FT - 1)).then_inc(s_oe, 1)

            def transpose_gates(k):
                if k == 0:
                    pe.wait_ge(s_gsteps, GATES_MADE)
                after(pe, s_gatesT_sb, k - 1)
                for n in range(TPB):
                    ins = pe.transpose((b2_ps, fin_ps)[k % 2][0:E, n * N:(n + 1) * N], gates[:, TPB * k + n, :], ident[:, :])
                ins.then_inc(s_gatesT, 1)

            def transpose_sum(k):
                pe.wait_ge(s_acc, at(E * (k + 1)))
                for n in range(TPB):
                    ins = pe.transpose(fin_ps[:, n * N:(n + 1) * N], acc[:, n * N:(n + 1) * N], ident[:, :])
                ins.then_inc(s_fin, 1)

            def block_of(k, first):
                for s in range(E * FT):
                    hidden(k, s)
                    if s >= 2:
                        expert_out(k, s - 2)
                    elif not first:
                        expert_out(k - 1, E * FT - 2 + s)
                    if first and s < TPB:
                        transpose_gates(s)
                    if s == 4:
                        pe.wait_ge(s_gatesT_sb, TPB)
                        after(pe, s_acc, E * (k - 1) + 1)
                        pe.matmul(b2_ps, b2_rows[:, :], gatesT[:, bass.ds(at(BLOCK * k), BLOCK)], start=True,
                                  stop=True).then_inc(s_b2, 1)
                    if s == 5 and not first:
                        transpose_sum(k - 1)

            block_of(0, True)
            with pe.Fori(0, NBLOCKS - 1) as k:
                block_of(Count(k, 1, 1), False)
            k = NBLOCKS - 1
            expert_out(k, E * FT - 2)
            expert_out(k, E * FT - 1)
            transpose_sum(k)


X2T_CREDIT = 2
CONSTS = 16 * 14
GATE_DIFF = 4
GATES_MADE = 12

_INS = ['x', 'ctx_1024', 'L0_attn_ln_gamma', 'L0_attn_ln_beta', 'L0_attn_w_qkv', 'L0_attn_w_out', 'L0_attn_b_out',
        'L0_ffn_gate_w', 'L0_ffn_gate_b', 'L0_ffn_w1', 'L0_ffn_b1', 'L0_ffn_w2', 'L0_ffn_b2', 'L0_ffn_ln_g',
        'L0_ffn_ln_b']


def shape_constants():
    import numpy as np
    inv = (1.0 / 10000.0 ** (np.arange(0, HD, 2, dtype=np.float32) / np.float32(HD))).astype(np.float32)
    angle = np.arange(N, dtype=np.float32)[:, None] * inv[None, :]
    sin, cos = np.sin(angle), np.cos(angle)
    table = np.stack([np.concatenate([cos, cos], 1), np.concatenate([sin, -sin], 1)], 1)
    rope = np.stack([table * np.float32(HD ** -0.5), table], 1).astype(np.float32)
    masks = np.zeros((3, 128, 128), np.float32)
    masks[0] = np.eye(128)
    masks[1] = np.triu(np.ones((128, 128)), 1) * -1e10
    masks[2] = np.arange(128)[None, :]
    return {"rope": rope, "masks": masks}


def kernel(**inputs):
    import numpy as _np
    import concourse.bacc as _bacc
    from concourse import mybir as _mybir
    from concourse.bass_utils import run_bass_kernel_spmd as _run

    nc = _bacc.Bacc("TRN2", target_bir_lowering=False, num_devices=1)
    arrays, args = {}, []
    given = [(name, _np.ascontiguousarray(inputs[name])) for name in _INS] + list(shape_constants().items())
    for name, a in given:
        arrays[f"in_{name}_dram"] = a
        args.append(nc.dram_tensor(f"in_{name}_dram", a.shape, _mybir.dt.from_np(a.dtype), kind="ExternalInput").ap())
    args.append(nc.dram_tensor("out_0_dram", (B, N, D), F32, kind="ExternalOutput").ap())
    decoder_kernel(nc, *args)
    r = _run(nc, [arrays], core_ids=[0])
    return r.results[0]["out_0_dram"]
```

```python
from contextlib import ExitStack

import concourse.bass as bass
from concourse import mybir

F32 = mybir.dt.float32
F32R = mybir.dt.float32r
U32 = mybir.dt.uint32
ALU = mybir.AluOpType
ACT = mybir.ActivationFunctionType
AX = mybir.AxisListType

B, N, D = 16, 128, 128
H, HD = 16, 64
PAIRS = H // 2
QUADS = H // 4
E, F = 8, 512
FT = F // 128
CHUNK = 512
BLOCK = 512
NBLOCKS = B * N // BLOCK
TPB = BLOCK // N
WCOLS = E * F // B
EPS = 1e-5
INV_TEMP = 1.0 / 0.9
CROSS_SCALE = float(D) ** -0.5

CHUNKS = [0, 2 * CHUNK, CHUNK, 3 * CHUNK, 4 * CHUNK, 5 * CHUNK]
ROPE_CHUNKS = 4
COS, SIN = 0, 1


def head_of(t, j):
    return 4 * (t // 2) + j, t % 2


def made(count, most):
    return min(count, most) if isinstance(count, int) else count


class Count:

    def __init__(self, register, times=1, plus=0):
        self.register, self.times, self.plus = register, times, plus

    def __add__(self, n):
        return Count(self.register, self.times, self.plus + n)

    def __sub__(self, n):
        return self + -n

    def __mul__(self, n):
        return Count(self.register, self.times * n, self.plus * n)

    __radd__, __rmul__ = __add__, __mul__


def at(n):
    if isinstance(n, int):
        return n
    value = n.register * n.times if n.times != 1 else n.register
    return value + n.plus if n.plus else value


class Turn:

    def __init__(self, i, parity):
        self.i, self.parity, self.b = i, parity, 2 * i + parity

    def has(self, k):
        return not isinstance(self.b, int) or 0 <= self.b + k < B

    def ring(self, k):
        return (self.parity + k) % 2


def turns(eng, iteration):
    for b in range(-3, 4):
        iteration(Turn(b // 2, b % 2))
    with eng.Fori(0, B // 2 - 4) as i:
        iteration(Turn(Count(i, 1, 2), 0))
        iteration(Turn(Count(i, 1, 2), 1))
    for b in range(B - 4, B + 3):
        iteration(Turn(b // 2, b % 2))


def after(eng, sem, count):
    if not isinstance(count, int) or count > 0:
        eng.wait_ge(sem, at(count))


def decoder_kernel(nc, x, ctx_kv, ln_gamma, ln_beta, w_qkv, w_out, b_out, gate_w, gate_b,
                   w1, b1, w2, b2, ffn_g, ffn_b, rope, masks, out):
    with ExitStack() as stack:
        def sb(name, shape, dt=F32):
            return stack.enter_context(nc.sbuf_tensor(name, shape, dt))

        def sem(name):
            return stack.enter_context(nc.semaphore(name))

        gates_dram = nc.dram_tensor("gates_by_expert", (E, B * N), F32, kind="Internal").ap()

        ps = stack.enter_context(nc.psum_tensor("ps", [128, 8, 512], F32))
        proj_ps = [ps[:, 0, :], ps[:, 1, :]]
        turn_ps = ps[:, 2, :]
        score_ps = [ps[:, 3, :], ps[:, 4, :]]
        probsT_ps = ps[:, 5, :]
        pv_ps = ps[:, 6, :]
        small_ps = ps[:, 7, 0:N]
        h_ps = [ps[:, n, :] for n in range(4)]
        oe_ps = [ps[:, 4, :], ps[:, 5, :]]
        b2_ps = ps[:, 6, :]
        fin_ps = ps[:, 7, :]

        ident = sb("ident", [128, 128])
        cmask = sb("cmask", [128, 128])
        iota8 = sb("iota8", [128, E])
        ropes = sb("ropes", [128, 2, 2, HD])
        vec_rows = sb("vec_rows", [2 + E * FT, 128])
        vec_cols = sb("vec_cols", [128, 2 + E * FT])
        gamma, beta = vec_cols[:, 0:1], vec_cols[:, 1:2]
        bout_bc = sb("bout_bc", [128, D])
        gateb_bc = sb("gateb_bc", [128, E])
        ffng_bc = sb("ffng_bc", [128, D])
        ffnb_bc = sb("ffnb_bc", [128, D])
        gatew = sb("gatew", [128, E])
        b2_rows = sb("b2_rows", [E, D])
        half = sb("half", [128, 1])
        hold = sb("hold", [128, 1])
        wqkv_hi = sb("wqkv_hi", [128, 6, CHUNK], F32R)
        wqkv_lo = sb("wqkv_lo", [128, 6, CHUNK], F32R)
        wout = sb("wout", [128, PAIRS, D])
        w_stage = sb("w_stage", [128, 2, 2, WCOLS])
        w_hi = sb("w_hi", [128, 2, E * F], F32R)
        w_lo = sb("w_lo", [128, 2, E * F], F32R)

        x_all = sb("x_all", [128, B, D])
        ctx_in = sb("ctx_in", [128, 2, D])
        xc = sb("xc", [128, 2, D])
        xn_f = sb("xn_f", [128, 2, N])
        xn_hi = sb("xn_hi", [128, 2, N], F32R)
        xn_lo = sb("xn_lo", [128, 2, N], F32R)
        rope_cos = sb("rope_cos", [128, 2, CHUNK])
        rope_sin = sb("rope_sin", [128, 2, CHUNK])
        rot = sb("rot", [128, 2, CHUNK])
        rotT = sb("rotT", [128, 2, 2, PAIRS, N])
        v_sb = sb("v_sb", [128, 2, H * HD])
        probs = sb("probs", [128, QUADS, 4, N])
        negmax = sb("negmax", [128, QUADS, 4])
        den = sb("den", [128, QUADS, 4])
        rden = sb("rden", [128, QUADS, 4])
        probsT = sb("probsT", [128, 2, 4, N])
        headsT = sb("headsT", [128, 2, PAIRS, N])
        y1 = sb("y1", [128, D])
        x1 = sb("x1", [128, 2, D])
        x1ctxT = sb("x1ctxT", [128, 2, N])
        cdots = sb("cdots", [128, N])
        cprobs = sb("cprobs", [128, N])
        cprobsT = sb("cprobsT", [128, N])
        cneg = sb("cneg", [128, 2])
        cden = sb("cden", [128, 2])
        y2 = sb("y2", [128, D])
        x2 = sb("x2", [128, 2, D])
        x2T = sb("x2T", [128, B * N])
        x2T_hi = sb("x2T_hi", [128, B * N], F32R)
        x2T_lo = sb("x2T_lo", [128, B * N], F32R)

        wqkv_in = [x2T[:, c * CHUNK:(c + 1) * CHUNK] for c in range(4)] + [
            v_sb[:, 1, j * CHUNK:(j + 1) * CHUNK] for j in range(2)]

        g_f = [rope_cos[:, n, :] for n in range(2)]
        g_hi = wqkv_hi[:, 0:4, :]
        g_lo = wqkv_lo[:, 0:4, :]
        gates_bc = rotT[:, :, :, :, :].rearrange("p r q a b -> p (r q a b)").rearrange("p (e n) -> p e n", e=E)
        weighted = [probs[:, n, :, :].rearrange("p a b -> p (a b)") for n in range(2)]
        acc = probs[:, 2, :, :].rearrange("p a b -> p (a b)")
        logits = sb("logits", [128, B, E])
        top = sb("top", [128, B, 8])
        top_at = sb("top_at", [128, B, 8], U32)
        top_atf = sb("top_atf", [128, B, 2])
        pair_g = sb("pair_g", [128, 4, B])
        hot = sb("hot", [128, 2, B, E])
        gates = sb("gates", [128, B, E])
        gatesT = headsT[0:E, :, :, :].rearrange("p r a b -> p (r a b)")
        z1 = v_sb[:, 0, 0:BLOCK].rearrange("p (t d) -> p t d", t=TPB)
        z2 = v_sb[:, 0, BLOCK:2 * BLOCK].rearrange("p (t d) -> p t d", t=TPB)
        res = v_sb[:, 1, 0:BLOCK].rearrange("p (t d) -> p t d", t=TPB)

        class Norm:

            def __init__(self, name, tiles=1):
                self.stats = sb(name + "_stats", [128, tiles, 6])
                self.mv = sb(name + "_mv", [128, tiles, 2])
                self.veps = sb(name + "_veps", [128, tiles])
                self.rstd = sb(name + "_rstd", [128, tiles])
                self.s_stats = sem(name + "_stats_made")
                self.s_mv = sem(name + "_moments_made")
                self.s_veps = sem(name + "_veps_made")
                self.s_rstd = sem(name + "_rstd_made")

            def moments(self, dve, tiles, n):
                k = len(tiles)
                for t, tile in enumerate(tiles):
                    dve.bn_stats(self.stats[:, t, :], tile).then_inc(self.s_stats, 1)
                dve.wait_ge(self.s_stats, at(k * n))
                dve.memset(hold[:, :], 0.0)
                for t in range(k):
                    dve.bn_aggr(self.mv[:, t, :], self.stats[:, t, :]).then_inc(self.s_mv, 1)
                dve.wait_ge(self.s_mv, at(k * n))
                dve.tensor_scalar(self.veps[:, 0:k], self.mv[:, :, 1], EPS, None,
                                  ALU.add).then_inc(self.s_veps, 1)

            def root(self, pool, n):
                pool.wait_ge(self.s_veps, at(n))
                k = self.rstd.shape[1]
                pool.tensor_tensor(self.rstd[:, :], self.veps[:, :], half[:, :].to_broadcast([128, k]),
                                   ALU.pow).then_inc(self.s_rstd, 1)

        norm_x, norm_1, norm_2 = Norm("norm_x"), Norm("norm_1"), Norm("norm_2")
        norm_f, norm_3 = Norm("norm_f", TPB), Norm("norm_3", TPB)

        s_x = [sem("x_first_loaded"), sem("x_rest_loaded")]
        s_first = sem("ident_and_vectors_loaded")
        s_rope = sem("rope_tables_loaded")
        s_const = sem("other_consts_loaded")
        s_wqkv = [sem(f"wqkv_chunk_{c}_loaded") for c in range(6)]
        s_ctx = [sem("ctx_even_loaded"), sem("ctx_odd_loaded")]
        s_w = [sem("w_even_loaded"), sem("w_odd_loaded")]
        s_turned = sem("three_transposed")
        s_x2T = sem("x2_transposed")
        s_proj = sem("proj_made")
        s_rotT = sem("rot_transposed")
        s_scores = sem("scores_made")
        s_probsT = sem("probs_transposed")
        s_pv = sem("pv_made")
        s_attn = sem("attn_out_made")
        s_dots = sem("cross_dots_made")
        s_cprobsT = sem("cross_probs_transposed")
        s_cross = sem("cross_out_made")
        s_vecT = sem("vec_transposed")
        s_vec = sem("vec_cols_made")
        s_half = sem("half_set")
        s_wqkv_lo = [sem("wqkv_even_lo_made"), sem("wqkv_odd_lo_made")]
        s_xc = sem("xc_made")
        s_roped = sem("rope_products_made")
        s_negmax = sem("negmax_made")
        s_rden = sem("rden_made")
        s_heads = sem("heads_copied")
        s_y1 = sem("y1_made")
        s_x1 = sem("x1_made")
        s_cdots = sem("cross_dots_masked")
        s_cmax = sem("cross_max_made")
        s_cneg = sem("cross_negmax_made")
        s_crden = sem("cross_rden_made")
        s_y2 = sem("y2_made")
        s_x2 = sem("x2_made")
        s_wqkv_hi = sem("wqkv_hi_made")
        s_xn = sem("xn_made")
        s_rotT_sb = sem("rotT_copied")
        s_v = sem("v_copied")
        s_exp = sem("exp_made")
        s_probsT_sb = sem("probsT_copied")
        s_x1ctxT_sb = sem("x1ctxT_copied")
        s_cexp = sem("cross_exp_made")
        s_cprobsT_sb = sem("cross_probsT_copied")
        s_x2T_sb = sem("x2T_copied")
        s_w_hi = sem("w_hi_made")
        s_rot = sem("rot_made")
        s_probs = sem("probs_normalised")
        s_biased = sem("x_biased")
        s_xn_lo = sem("xn_lo_made")
        s_x2_kept = sem("x2_kept")
        s_x2_lo = sem("x2_lo_made")
        s_w_lo = sem("w_lo_made")
        s_logits = sem("logits_made")
        s_gsteps = sem("gating_steps_done")
        s_gexp = sem("gate_exp_made")
        s_gatesT = sem("gates_transposed")
        s_gatesT_sb = sem("gatesT_copied")
        s_gates_out = sem("gates_stored")
        s_gbc = [sem(f"gates_bc_loaded_{e}") for e in range(E)]
        s_h = sem("hidden_made")
        s_gelu = sem("gelu_made")
        s_g_lo = sem("gelu_lo_made")
        s_oe = sem("expert_out_made")
        s_b2 = sem("b2_part_made")
        s_weighted = sem("expert_weighted")
        s_acc = sem("experts_summed")
        s_fin = sem("moe_transposed")
        s_z = sem("ffn_normalised")
        s_affine = sem("ffn_affine_made")
        s_res = sem("final_normalised")
        s_out = sem("out_stored")

        block = stack.enter_context(nc.Block())

        def bcast(v):
            return v.rearrange("(a n) -> a n", a=1).to_broadcast([128, v.shape[0]])

        def store(sp, k):
            sp.wait_ge(s_res, at(k + 1))
            sp.dma_start(out[bass.ds(at(TPB * k), TPB)].rearrange("b p d -> p b d"), res).then_inc(s_out, 16)

        @block.sync
        def _(sp):
            sp.sem_inc(s_out, 16)
            x_t = x.rearrange("b p d -> p b d")
            sp.dma_start(x_all[:, 0:2, :], x_t[:, 0:2, :]).then_inc(s_x[0], 16)
            for c, col in enumerate(CHUNKS):
                sp.dma_start(wqkv_in[c], w_qkv[:, col:col + CHUNK]).then_inc(s_wqkv[c], 16)
            sp.dma_start(x_all[:, 2:B, :], x_t[:, 2:B, :]).then_inc(s_x[1], 16)
            others = [(bout_bc[:, :], bcast(b_out)), (wout[:, :, :], w_out.rearrange("(t p) d -> p t d", p=128)),
                      (cmask[:, :], masks[1]), (iota8[:, :], masks[2][:, 0:E]), (gateb_bc[:, :], bcast(gate_b)),
                      (ffng_bc[:, :], bcast(ffn_g)), (ffnb_bc[:, :], bcast(ffn_b)), (gatew[:, :], gate_w),
                      (b2_rows[:, :], b2)]
            assert 16 * len(others) == CONSTS
            for dst, src in others:
                sp.dma_start(dst, src).then_inc(s_const, 16)

            def iteration(t):
                if t.has(0):
                    r, b = t.ring(0), t.b
                    after(sp, s_w_lo, b - 1)
                    sp.dma_start(w_stage[:, r, 0, :],
                                 w1[at(t.i), :, r * WCOLS:(r + 1) * WCOLS]).then_inc(s_w[r], 16)
                    sp.dma_start(w_stage[:, r, 1, :].rearrange("p (f d) -> p f d", d=D),
                                 w2[at(t.i), r * 2 * 128:(r + 1) * 2 * 128, :].rearrange("(f p) d -> p f d", p=128)
                                 ).then_inc(s_w[r], 16)
                if t.has(-1):
                    r = t.ring(-1)
                    after(sp, s_cross, t.b - 2)
                    sp.dma_start(ctx_in[:, r, :], ctx_kv[at(t.b - 1)]).then_inc(s_ctx[r], 16)

            turns(sp, iteration)

            sp.wait_ge(s_gatesT_sb, TPB)
            sp.dma_start(gates_dram, gatesT[:, :]).then_inc(s_gates_out, 16)
            sp.wait_ge(s_gates_out, 16)

            def gates_of(k):
                for e in range(E):
                    after(sp, s_weighted, E * (k - 1) + e + 1)
                    sp.dma_start(gates_bc[:, e, :],
                                 gates_dram[e:e + 1, bass.ds(at(BLOCK * k), BLOCK)].to_broadcast([128, BLOCK])
                                 ).then_inc(s_gbc[e], 16)

            gates_of(0)
            with sp.Fori(0, NBLOCKS - 1) as k:
                gates_of(Count(k, 1, 1))
                store(sp, Count(k))
            store(sp, NBLOCKS - 1)
            sp.wait_ge(s_out, 16 * (NBLOCKS + 1))

        @block.scalar
        def _(act):
            for dst, src in [(ident[:, :], masks[0]), (vec_rows[0:1, :], ln_gamma.rearrange("(a n) -> a n", a=1)),
                             (vec_rows[1:2, :], ln_beta.rearrange("(a n) -> a n", a=1)),
                             (vec_rows[2:2 + E * FT, :], b1.rearrange("e (f p) -> (e f) p", p=128))]:
                act.dma_start(dst, src).then_inc(s_first, 16)
            act.dma_start(ropes[:, :, :, :], rope).then_inc(s_rope, 16)

            def wqkv_high(c):
                act.wait_ge(s_wqkv[c], 16)
                act.activation(wqkv_hi[:, c, :], wqkv_in[c], ACT.Copy).then_inc(s_wqkv_hi, 1)

            wqkv_high(0)
            wqkv_high(1)
            act.wait_ge(s_vec, 1)

            def exps(b, t):
                act.wait_ge(s_negmax, at(4 * b + t + 1))
                after(act, s_probsT, 4 * (b - 1) + t + 1)
                for h in range(4):
                    e = act.activation(probs[:, t, h, :], score_ps[t % 2][:, h * N:(h + 1) * N], ACT.Exp,
                                       bias=negmax[:, t, h:h + 1], accum_out=den[:, t, h:h + 1])
                e.then_inc(s_exp, 1)

            def probsT_copy(b, t):
                act.wait_ge(s_probsT, at(4 * b + t + 1))
                after(act, s_pv, 2 * b + t // 2)
                act.activation(probsT[:, t % 2, :, :].rearrange("p a b -> p (a b)"), probsT_ps,
                               ACT.Copy).then_inc(s_probsT_sb, 1)

            def rotT_copy(b, r, c):
                act.wait_ge(s_rotT, at(4 * b + c + 1))
                act.activation(rotT[:, r, c % 2, 4 * (c // 2):4 * (c // 2) + 4, :],
                               turn_ps.rearrange("p (a b) -> p a b", a=4), ACT.Copy).then_inc(s_rotT_sb, 1)

            def iteration(t):
                b = t.b
                if t.has(-1):
                    probsT_copy(b - 1, 2)
                if t.has(0):
                    rotT_copy(b, t.ring(0), 2)
                    exps(b, 0)
                if t.has(-2) or t.has(2):
                    act.wait_ge(s_turned, at(b + 3))
                if t.has(-2):
                    act.activation(x1ctxT[:, :, :].rearrange("p a b -> p (a b)"), turn_ps[:, 0:2 * N],
                                   ACT.Copy).then_inc(s_x1ctxT_sb, 1)
                if t.has(2):
                    after(act, s_proj, 6 * (b + 1))
                    for xn in (xn_f, xn_hi):
                        act.activation(xn[:, t.ring(2), :], turn_ps[:, 2 * N:3 * N], ACT.Identity, bias=beta,
                                       scale=gamma).then_inc(s_xn, 1)
                if isinstance(b, int) and b == -2:
                    for c in range(2, 6):
                        wqkv_high(c)
                if t.has(-1):
                    probsT_copy(b - 1, 3)
                if t.has(0):
                    rotT_copy(b, t.ring(0), 3)
                    exps(b, 1)
                if t.has(0):
                    probsT_copy(b, 0)
                if t.has(1):
                    rotT_copy(b + 1, t.ring(1), 0)
                if t.has(0):
                    exps(b, 2)
                if t.has(-2):
                    act.wait_ge(s_cneg, at(b - 1))
                    act.activation(cprobs[:, :], cdots[:, :], ACT.Exp, bias=cneg[:, 1:2], scale=CROSS_SCALE,
                                   accum_out=cden[:, 0:1]).then_inc(s_cexp, 1)
                if t.has(-3):
                    act.wait_ge(s_x2T, at(b - 2))
                    for x2_turned in (x2T, x2T_hi):
                        act.activation(x2_turned[:, bass.ds(at((b - 3) * N), N)], turn_ps[:, 0:N],
                                       ACT.Copy).then_inc(s_x2T_sb, 1)
                if t.has(0):
                    probsT_copy(b, 1)
                if t.has(1):
                    rotT_copy(b + 1, t.ring(1), 1)
                if t.has(0):
                    exps(b, 3)
                if t.has(-2):
                    act.wait_ge(s_cprobsT, at(b - 1))
                    act.activation(cprobsT[:, :], turn_ps[:, 0:N], ACT.Copy).then_inc(s_cprobsT_sb, 1)
                if t.has(1):
                    after(act, s_pv, 2 * b)
                    for j in range(2):
                        act.wait_ge(s_proj, at(6 * (b + 1) + 5 + j))
                        act.activation(v_sb[:, t.ring(1), j * CHUNK:(j + 1) * CHUNK], proj_ps[j],
                                       ACT.Copy).then_inc(s_v, 1)
                if t.has(0):
                    act.wait_ge(s_w[t.ring(0)], at(32 * (t.i + 1)))
                    act.activation(w_hi[:, :, bass.ds(at(b * WCOLS), WCOLS)], w_stage[:, t.ring(0), :, :],
                                   ACT.Copy).then_inc(s_w_hi, 1)

            turns(act, iteration)

            act.wait_ge(s_gsteps, GATE_DIFF)
            act.activation(pair_g[:, 1, :], pair_g[:, 0, :], ACT.Exp).then_inc(s_gexp, 1)

            def block_of(k):
                for s in range(E * FT):
                    act.wait_ge(s_h, at(E * FT * k + s + 1))
                    after(act, s_g_lo, E * FT * k + s - 1)
                    after(act, s_oe, E * FT * k + s - 3)
                    b1_col = vec_cols[:, 2 + s:3 + s]
                    act.activation(g_f[s % 2], h_ps[s % 4], ACT.Gelu, bias=b1_col).then_inc(s_gelu, 1)
                    act.activation(g_hi[:, s % 4, :], h_ps[s % 4], ACT.Gelu,
                                   bias=b1_col).then_inc(s_gelu, 1)

            block_of(0)
            with act.Fori(0, NBLOCKS - 1) as k:
                block_of(Count(k, 1, 1))

        @block.gpsimd
        def _(pool):
            pool.wait_ge(s_half, 1)

            def wqkv_low(c):
                pool.wait_ge(s_wqkv_hi, c + 1)
                pool.tensor_tensor(wqkv_lo[:, c, :], wqkv_in[c], wqkv_hi[:, c, :],
                                   ALU.subtract).then_inc(s_wqkv_lo[1], 1)

            def rotate(b, c):
                pool.wait_ge(s_roped, at(4 * b + c + 1))
                after(pool, s_rotT, 4 * b + c - 1)
                o = rot[:, c % 2, :].rearrange("p (h s j) -> p h s j", s=2, j=HD // 2)
                co = rope_cos[:, c % 2, :].rearrange("p (h s j) -> p h s j", s=2, j=HD // 2)
                si = rope_sin[:, c % 2, :].rearrange("p (h s j) -> p h s j", s=2, j=HD // 2)
                pool.tensor_tensor(o[:, :, 0, :], co[:, :, 0, :], si[:, :, 1, :], ALU.add)
                pool.tensor_tensor(o[:, :, 1, :], co[:, :, 1, :], si[:, :, 0, :], ALU.add).then_inc(s_rot, 1)

            def normalise(b, t):
                pool.wait_ge(s_rden, at(4 * b + t + 1))
                pool.tensor_tensor(probs[:, t, :, :], probs[:, t, :, :],
                                   rden[:, t, :].unsqueeze(2).to_broadcast([128, 4, N]),
                                   ALU.mult).then_inc(s_probs, 1)

            def iteration(t):
                b = t.b
                if t.has(-1):
                    normalise(b - 1, 3)
                if t.has(-3):
                    norm_2.root(pool, b - 2)
                if t.has(1):
                    rotate(b + 1, 0)
                if t.has(0):
                    normalise(b, 0)
                if t.has(1):
                    rotate(b + 1, 1)
                if t.has(2):
                    pool.wait_ge(s_xn, at(2 * (b + 3)))
                    pool.tensor_tensor(xn_lo[:, t.ring(2), :], xn_f[:, t.ring(2), :], xn_hi[:, t.ring(2), :],
                                       ALU.subtract).then_inc(s_xn_lo, 1)
                if t.has(-3):
                    pool.wait_ge(s_x2, at(b - 2))
                    pool.tensor_copy(x_all[:, bass.ds(at(b - 3), 1), :], x2[:, t.ring(-3), :].unsqueeze(1)).then_inc(s_x2_kept, 1)
                if t.has(0):
                    normalise(b, 1)
                if t.has(3):
                    norm_x.root(pool, b + 4)
                if isinstance(b, int) and b == -3:
                    wqkv_low(1)
                if isinstance(b, int) and b == -2:
                    wqkv_low(3)
                    wqkv_low(5)
                if t.has(1):
                    rotate(b + 1, 2)
                if t.has(-1):
                    norm_1.root(pool, b)
                if t.has(0):
                    normalise(b, 2)
                if t.has(-3):
                    pool.wait_ge(s_x2T_sb, at(2 * (b - 2)))
                    pool.tensor_tensor(x2T_lo[:, bass.ds(at((b - 3) * N), N)], x2T[:, bass.ds(at((b - 3) * N), N)],
                                       x2T_hi[:, bass.ds(at((b - 3) * N), N)], ALU.subtract).then_inc(s_x2_lo, 1)
                if t.has(1):
                    rotate(b + 1, 3)
                if t.has(3):
                    if isinstance(b, int) and b == -3:
                        pool.wait_ge(s_const, CONSTS)
                    pool.wait_ge(s_xc, at(b + 4))
                    pool.tensor_tensor(x_all[:, bass.ds(at(b + 3), 1), :], x_all[:, bass.ds(at(b + 3), 1), :],
                                       bout_bc[:, :].unsqueeze(1), ALU.add).then_inc(s_biased, 1)
                if t.has(0):
                    pool.wait_ge(s_w_hi, at(b + 1))
                    pool.tensor_tensor(w_lo[:, :, bass.ds(at(b * WCOLS), WCOLS)], w_stage[:, t.ring(0), :, :],
                                       w_hi[:, :, bass.ds(at(b * WCOLS), WCOLS)], ALU.subtract).then_inc(s_w_lo, 1)

            turns(pool, iteration)

            def sum_expert(k, e):
                pool.wait_ge(s_weighted, at(E * k + e + 1))
                pool.wait_ge(s_acc, at(E * k + e))
                pool.tensor_tensor(acc, acc, weighted[e % 2], ALU.add).then_inc(s_acc, 1)

            def finish(k):
                norm_f.root(pool, k + 1)
                pool.wait_ge(s_z, at(4 * k + 4))
                pool.tensor_tensor(z2, z1, ffng_bc[:, :].unsqueeze(1).to_broadcast([128, TPB, D]),
                                   ALU.mult).then_inc(s_affine, 1)
                pool.wait_ge(s_affine, at(3 * k + 1))
                pool.tensor_tensor(z2, z2, ffnb_bc[:, :].unsqueeze(1).to_broadcast([128, TPB, D]),
                                   ALU.add).then_inc(s_affine, 1)
                pool.wait_ge(s_affine, at(3 * k + 2))
                pool.tensor_tensor(z2, z2, x_all[:, bass.ds(at(TPB * k), TPB), :], ALU.add).then_inc(s_affine, 1)
                norm_3.root(pool, k + 1)

            def block_of(k, first):
                for e in range(1, E):
                    if e == 2 and not first:
                        finish(k - 1)
                    sum_expert(k, e)

            block_of(0, True)
            with pool.Fori(0, NBLOCKS - 1) as k:
                block_of(Count(k, 1, 1), False)
            finish(NBLOCKS - 1)

        @block.vector
        def _(dve):
            dve.memset(half[:, :], -0.5).then_inc(s_half, 1)

            def rope_products(b, c):
                dve.wait_ge(s_proj, at(6 * b + c + 1))
                after(dve, s_rot, 4 * b + c - 1)
                p = proj_ps[c % 2].rearrange("p (h j) -> p h j", j=HD)
                for kind, dst in ((COS, rope_cos), (SIN, rope_sin)):
                    table = ropes[:, c % 2, kind, :].unsqueeze(1).to_broadcast([128, CHUNK // HD, HD])
                    ins = dve.tensor_tensor(dst[:, c % 2, :].rearrange("p (h j) -> p h j", j=HD), p, table, ALU.mult)
                ins.then_inc(s_roped, 1)

            def row_max(b, t):
                dve.wait_ge(s_scores, at(4 * b + t + 1))
                dve.tensor_reduce(negmax[:, t, :], score_ps[t % 2].rearrange("p (h k) -> p h k", h=4), AX.X,
                                  ALU.max, negate=True).then_inc(s_negmax, 1)

            def recip(b, t):
                dve.wait_ge(s_exp, at(4 * b + t + 1))
                dve.reciprocal(rden[:, t, :], den[:, t, :]).then_inc(s_rden, 1)

            def heads_copy(b, r, o):
                dve.wait_ge(s_pv, at(2 * b + o + 1))
                dve.tensor_copy(headsT[:, r, 4 * o:4 * o + 4, :].rearrange("p a b -> p (a b)"),
                                pv_ps).then_inc(s_heads, 1)

            def normed(norm, n, dst, src):
                dve.wait_ge(norm.s_rstd, at(n))
                return dve.tensor_scalar(dst, src, norm.mv[:, 0, 0:1], norm.rstd[:, 0:1], ALU.subtract, ALU.mult)

            def wqkv_low(c):
                dve.wait_ge(s_wqkv_hi, c + 1)
                dve.tensor_tensor(wqkv_lo[:, c, :], wqkv_in[c], wqkv_hi[:, c, :],
                                  ALU.subtract).then_inc(s_wqkv_lo[0], 1)

            def iteration(t):
                b = t.b
                if t.has(0):
                    row_max(b, 0)
                if t.has(-1):
                    heads_copy(b - 1, t.ring(-1), 0)
                if t.has(-3):
                    dve.wait_ge(s_cross, at(b - 2))
                    dve.wait_ge(s_crden, at(b - 2))
                    dve.scalar_tensor_tensor(y2[:, :], small_ps, cden[:, 1:2], x1[:, t.ring(-3), :], ALU.mult,
                                             ALU.add).then_inc(s_y2, 1)
                    dve.wait_ge(s_y2, at(b - 2))
                    norm_2.moments(dve, [y2[:, :]], b - 2)
                if t.has(1):
                    rope_products(b + 1, 0)
                if t.has(0):
                    recip(b, 0)
                if t.has(0):
                    row_max(b, 1)
                if t.has(-3):
                    normed(norm_2, b - 2, x2[:, t.ring(-3), :], y2[:, :]).then_inc(s_x2, 1)
                if t.has(1):
                    rope_products(b + 1, 1)
                if t.has(0):
                    recip(b, 1)
                if t.has(-2):
                    dve.wait_ge(s_dots, at(b - 1))
                    dve.tensor_tensor(cdots[:, :], small_ps, cmask[:, :], ALU.add).then_inc(s_cdots, 1)
                    dve.wait_ge(s_cdots, at(b - 1))
                    dve.tensor_reduce(cneg[:, 0:1], cdots[:, :], AX.X, ALU.max, negate=True).then_inc(s_cmax, 1)
                    dve.wait_ge(s_cmax, at(b - 1))
                    dve.tensor_scalar(cneg[:, 1:2], cneg[:, 0:1], CROSS_SCALE, None, ALU.mult).then_inc(s_cneg, 1)
                if t.has(0):
                    row_max(b, 2)
                if t.has(-1):
                    heads_copy(b - 1, t.ring(-1), 1)
                if t.has(1):
                    rope_products(b + 1, 2)
                if t.has(3):
                    if isinstance(b, int):
                        dve.wait_ge(s_x[0 if b + 3 < 2 else 1], 16)
                    norm_x.moments(dve, [x_all[:, bass.ds(at(b + 3), 1), :].rearrange("p a d -> p (a d)")], b + 4)
                if t.has(0):
                    recip(b, 2)
                if t.has(1):
                    rope_products(b + 1, 3)
                if t.has(-1):
                    dve.wait_ge(s_attn, at(b))
                    dve.wait_ge(s_biased, at(b))
                    dve.tensor_tensor(y1[:, :], small_ps, x_all[:, bass.ds(at(b - 1), 1), :].rearrange("p a d -> p (a d)"),
                                      ALU.add).then_inc(s_y1, 1)
                    dve.wait_ge(s_y1, at(b))
                    norm_1.moments(dve, [y1[:, :]], b)
                if t.has(0):
                    row_max(b, 3)
                if t.has(3):
                    after(dve, s_turned, b + 2)
                    normed(norm_x, b + 4, xc[:, t.ring(3), :],
                           x_all[:, bass.ds(at(b + 3), 1), :].rearrange("p a d -> p (a d)")).then_inc(s_xc, 1)
                if t.has(-1):
                    normed(norm_1, b, x1[:, t.ring(-1), :], y1[:, :]).then_inc(s_x1, 1)
                if t.has(-2):
                    dve.wait_ge(s_cexp, at(b - 1))
                    dve.reciprocal(cden[:, 1:2], cden[:, 0:1]).then_inc(s_crden, 1)
                if t.has(0):
                    recip(b, 3)
                if isinstance(b, int) and b == -3:
                    dve.wait_ge(s_vecT, 1)
                    dve.tensor_copy(vec_cols[:, :], probsT_ps[:, 0:2 + E * FT]).then_inc(s_vec, 1)
                    wqkv_low(0)
                if isinstance(b, int) and b == -2:
                    wqkv_low(2)
                    wqkv_low(4)
                    dve.wait_ge(s_rope, 16)
                    dve.wait_ge(s_const, CONSTS)

            turns(dve, iteration)

            steps = [0]

            def step(ins):
                ins.then_inc(s_gsteps, 1)
                steps[0] += 1
                dve.wait_ge(s_gsteps, steps[0])

            dve.wait_ge(s_logits, 1)
            step(dve.tensor_tensor(logits[:, :, :], b2_ps[:, 0:B * E].rearrange("p (t e) -> p t e", e=E),
                                   gateb_bc[:, :].unsqueeze(1).to_broadcast([128, B, E]), ALU.add))
            step(dve.tensor_scalar(logits[:, :, :], logits[:, :, :], INV_TEMP, None, ALU.mult))
            for n in range(B):
                ins = dve.max(top[:, n, :], logits[:, n, :])
            step(ins)
            step(dve.tensor_tensor(pair_g[:, 0, :], top[:, :, 1], top[:, :, 0], ALU.subtract))
            assert steps[0] == GATE_DIFF
            for n in range(B):
                ins = dve.max_index(top_at[:, n, :], top[:, n, :], logits[:, n, :])
            step(ins)
            step(dve.tensor_copy(top_atf[:, :, :], top_at[:, :, 0:2]))
            for j in range(2):
                ins = dve.tensor_tensor(hot[:, j, :, :], iota8[:, :].unsqueeze(1).to_broadcast([128, B, E]),
                                        top_atf[:, :, j:j + 1].to_broadcast([128, B, E]), ALU.is_equal)
            step(ins)
            dve.wait_ge(s_gexp, 1)
            step(dve.tensor_scalar(pair_g[:, 0, :], pair_g[:, 1, :], 1.0, None, ALU.add))
            step(dve.reciprocal(pair_g[:, 2, :], pair_g[:, 0, :]))
            step(dve.tensor_tensor(pair_g[:, 3, :], pair_g[:, 1, :], pair_g[:, 2, :], ALU.mult))
            for j in range(2):
                ins = dve.tensor_tensor(hot[:, j, :, :], hot[:, j, :, :],
                                        pair_g[:, 2 + j, :].unsqueeze(2).to_broadcast([128, B, E]), ALU.mult)
            step(ins)
            step(dve.tensor_tensor(gates[:, :, :], hot[:, 0, :, :], hot[:, 1, :, :], ALU.add))
            assert steps[0] == GATES_MADE

            def gates_copy(k):
                dve.wait_ge(s_gatesT, at(k + 1))
                dve.tensor_copy(gatesT[:, k * BLOCK:(k + 1) * BLOCK],
                                (b2_ps, fin_ps)[k % 2][0:E, :]).then_inc(s_gatesT_sb, 1)

            def weigh(k, e):
                dve.wait_ge(s_oe, at(E * FT * k + FT * (e + 1)))
                dve.wait_ge(s_gbc[e], at(16 * (k + 1)))
                after(dve, s_acc, E * k + e - 1)
                dve.tensor_tensor(weighted[e % 2], oe_ps[e % 2], gates_bc[:, e, :], ALU.mult).then_inc(s_weighted, 1)
                if e == 0:
                    dve.wait_ge(s_weighted, at(E * k + 1))
                    dve.wait_ge(s_b2, at(k + 1))
                    after(dve, s_fin, k)
                    dve.tensor_tensor(acc, weighted[0], b2_ps, ALU.add).then_inc(s_acc, 1)

            def finish_stats(k):
                dve.wait_ge(s_fin, at(k + 1))
                norm_f.moments(dve, [fin_ps[:, n * N:(n + 1) * N] for n in range(TPB)], k + 1)

            def finish_norm(k):
                dve.wait_ge(norm_f.s_rstd, at(k + 1))
                for n in range(TPB):
                    dve.tensor_scalar(z1[:, n, :], fin_ps[:, n * N:(n + 1) * N], norm_f.mv[:, n, 0:1],
                                      norm_f.rstd[:, n:n + 1], ALU.subtract, ALU.mult).then_inc(s_z, 1)

            def finish_stats2(k):
                dve.wait_ge(s_affine, at(3 * k + 3))
                norm_3.moments(dve, [z2[:, n, :] for n in range(TPB)], k + 1)

            def finish_norm2(k):
                dve.wait_ge(norm_3.s_rstd, at(k + 1))
                dve.wait_ge(s_out, at(16 * (k + 1)))
                for n in range(TPB):
                    ins = dve.tensor_scalar(res[:, n, :], z2[:, n, :], norm_3.mv[:, n, 0:1],
                                            norm_3.rstd[:, n:n + 1], ALU.subtract, ALU.mult)
                ins.then_inc(s_res, 1)

            def block_of(k, first):
                for s in range(E * FT):
                    dve.wait_ge(s_gelu, at(2 * (E * FT * k + s) + 2))
                    after(dve, s_oe, E * FT * k + s - 3)
                    dve.tensor_tensor(g_lo[:, s % 4, :], g_f[s % 2], g_hi[:, s % 4, :],
                                      ALU.subtract).then_inc(s_g_lo, 1)
                    if first and s < TPB:
                        gates_copy(s)
                    if s % FT == 2 and s > FT:
                        weigh(k, s // FT - 1)
                    if not first:
                        if s == 2:
                            weigh(k - 1, E - 1)
                        if s == 9:
                            finish_stats(k - 1)
                        if s == 12:
                            finish_norm(k - 1)
                        if s == 17:
                            finish_stats2(k - 1)
                        if s == 20:
                            finish_norm2(k - 1)

            block_of(0, True)
            with dve.Fori(0, NBLOCKS - 1) as k:
                block_of(Count(k, 1, 1), False)
            k = NBLOCKS - 1
            weigh(k, E - 1)
            finish_stats(k)
            finish_norm(k)
            finish_stats2(k)
            finish_norm2(k)

        @block.tensor
        def _(pe):
            pe.wait_ge(s_first, 16 * 4)
            pe.transpose(probsT_ps[:, 0:2 + E * FT], vec_rows[:, :], ident[0:2 + E * FT, 0:2 + E * FT]).then_inc(s_vecT, 1)

            def project(b, r, c):
                if c == 0:
                    pe.wait_ge(s_xn_lo, at(b + 1))
                if c < 2:
                    after(pe, s_v, 2 * b + c - 1)
                else:
                    pe.wait_ge(s_roped, at(4 * b + c - 1))
                if isinstance(b, int) and b == 0:
                    pe.wait_ge(s_wqkv_lo[c % 2], c // 2 + 1)
                pe.matmul(proj_ps[c % 2], xn_hi[:, r, :], wqkv_hi[:, c, :], start=True, stop=False)
                pe.matmul(proj_ps[c % 2], xn_hi[:, r, :], wqkv_lo[:, c, :], start=False, stop=False)
                pe.matmul(proj_ps[c % 2], xn_lo[:, r, :], wqkv_hi[:, c, :], start=False,
                          stop=True).then_inc(s_proj, 1)

            def turned_copied(b):
                after(pe, s_x1ctxT_sb, made(b - 1, B))
                after(pe, s_xn, made(2 * (b + 3), 2 * B))

            def transpose_rot(b, c):
                pe.wait_ge(s_rot, at(4 * b + c + 1))
                after(pe, s_rotT_sb, 4 * b + c)
                if c == 0 and isinstance(b, int):
                    turned_copied(b - 1)
                if c == 1:
                    after(pe, s_x2T_sb, 2 * (b - 3))
                if c == 2:
                    after(pe, s_cprobsT_sb, b - 2)
                if c == 3:
                    turned_copied(b)
                for p in range(4):
                    ins = pe.transpose(turn_ps[:, p * N:(p + 1) * N], rot[:, c % 2, p * 128:(p + 1) * 128], ident[:, :])
                ins.then_inc(s_rotT, 1)

            def turn_three(t):
                b = t.b
                after(pe, s_rotT_sb, made(4 * b + 3, 4 * B))
                if isinstance(b, int):
                    after(pe, s_cprobsT_sb, made(b - 2, B))
                    turned_copied(b - 1)
                if t.has(-2):
                    pe.wait_ge(s_x1, at(b - 1))
                    pe.wait_ge(s_ctx[t.ring(-2)], at(16 * t.i))
                    pe.transpose(turn_ps[:, 0:N], x1[:, t.ring(-2), :], ident[:, :])
                    ins = pe.transpose(turn_ps[:, N:2 * N], ctx_in[:, t.ring(-2), :], ident[:, :])
                if t.has(2):
                    pe.wait_ge(s_xc, at(b + 3))
                    ins = pe.transpose(turn_ps[:, 2 * N:3 * N], xc[:, t.ring(2), :], ident[:, :])
                ins.then_inc(s_turned, 1)

            def scores(b, r, t):
                pe.wait_ge(s_rotT_sb, at(4 * b + (2 if t < 2 else 4)))
                after(pe, s_exp, 4 * b + t - 1)
                for j in range(4):
                    pair, side = head_of(t, j)
                    rows = slice(HD * side, HD * side + HD)
                    ins = pe.matmul(score_ps[t % 2][:, j * N:(j + 1) * N], rotT[rows, r, 0, pair, :],
                                    rotT[rows, r, 1, pair, :], start=True, stop=True)
                ins.then_inc(s_scores, 1)

            def transpose_probs(b, t):
                pe.wait_ge(s_probs, at(4 * b + t + 1))
                after(pe, s_probsT_sb, 4 * b + t)
                for j in range(4):
                    ins = pe.transpose(probsT_ps[:, j * N:(j + 1) * N], probs[:, t, j, :], ident[:, :])
                ins.then_inc(s_probsT, 1)

            def values(b, r, o):
                pe.wait_ge(s_probsT_sb, at(4 * b + 2 * o + 2))
                pe.wait_ge(s_v, at(2 * b + 2))
                after(pe, s_heads, 2 * b + o)
                for j in range(8):
                    quad = 2 * o + j % 2
                    pair, side = head_of(quad, j // 2)
                    h = 2 * pair + side
                    ins = pe.matmul(pv_ps[HD * side:HD * side + HD, (j // 2) * N:(j // 2 + 1) * N],
                                    v_sb[:, r, h * HD:(h + 1) * HD], probsT[:, quad % 2, j // 2, :],
                                    start=True, stop=True)
                ins.then_inc(s_pv, 1)

            def iteration(t):
                b = t.b
                if t.has(0):
                    scores(b, t.ring(0), 0)
                if t.has(-1):
                    values(b - 1, t.ring(-1), 0)
                    transpose_probs(b - 1, 2)
                if t.has(0):
                    transpose_rot(b, 2)
                if t.has(-3):
                    pe.wait_ge(s_cprobsT_sb, at(b - 2))
                    after(pe, s_y1, made(b - 1, B))
                    pe.matmul(small_ps, cprobsT[:, :], ctx_in[:, t.ring(-3), :], start=True, stop=True).then_inc(s_cross, 1)
                if t.has(1):
                    project(b + 1, t.ring(1), 0)
                if t.has(1):
                    project(b + 1, t.ring(1), 1)
                if t.has(-2) or t.has(2):
                    turn_three(t)
                if t.has(0):
                    scores(b, t.ring(0), 1)
                if t.has(-1):
                    transpose_probs(b - 1, 3)
                if t.has(0):
                    transpose_rot(b, 3)
                if t.has(-2):
                    pe.wait_ge(s_x1ctxT_sb, at(b - 1))
                    after(pe, s_y2, b - 2)
                    pe.matmul(small_ps, x1ctxT[:, 0, :], x1ctxT[:, 1, :], start=True, stop=True).then_inc(s_dots, 1)
                if t.has(1):
                    project(b + 1, t.ring(1), 2)
                if t.has(0):
                    scores(b, t.ring(0), 2)
                if t.has(-1):
                    values(b - 1, t.ring(-1), 1)
                if t.has(0):
                    transpose_probs(b, 0)
                if t.has(1):
                    transpose_rot(b + 1, 0)
                    project(b + 1, t.ring(1), 3)
                if t.has(-1):
                    pe.wait_ge(s_heads, at(2 * b))
                    after(pe, s_cdots, b - 1)
                    if isinstance(b, int) and b == 1:
                        pe.wait_ge(s_const, CONSTS)
                    for p in range(PAIRS):
                        ins = pe.matmul(small_ps, headsT[:, t.ring(-1), p, :], wout[:, p, :], start=(p == 0),
                                        stop=(p == PAIRS - 1))
                    ins.then_inc(s_attn, 1)
                if t.has(-3):
                    pe.wait_ge(s_x2, at(b - 2))
                    after(pe, s_rotT_sb, made(4 * (b + 1) + 1, 4 * B))
                    if isinstance(b, int):
                        turned_copied(b)
                    pe.transpose(turn_ps[:, 0:N], x2[:, t.ring(-3), :], ident[:, :]).then_inc(s_x2T, 1)
                if t.has(0):
                    scores(b, t.ring(0), 3)
                    transpose_probs(b, 1)
                if t.has(1):
                    transpose_rot(b + 1, 1)
                    project(b + 1, t.ring(1), 4)
                    project(b + 1, t.ring(1), 5)
                if t.has(-2):
                    pe.wait_ge(s_cexp, at(b - 1))
                    after(pe, s_rotT_sb, made(4 * (b + 1) + 2, 4 * B))
                    after(pe, s_x2T_sb, 2 * (b - 2))
                    pe.transpose(turn_ps[:, 0:N], cprobs[:, :], ident[:, :]).then_inc(s_cprobsT, 1)

            turns(pe, iteration)

            pe.wait_ge(s_x2T_sb, 2 * B)
            for n in range(B):
                ins = pe.matmul(b2_ps[:, n * E:(n + 1) * E], x2T[:, n * N:(n + 1) * N], gatew[:, :], start=True, stop=True)
            ins.then_inc(s_logits, 1)
            pe.wait_ge(s_x2_lo, B)
            pe.wait_ge(s_w_lo, B)

            def hidden(k, s):
                e, f = s // FT, s % FT
                after(pe, s_gelu, 2 * (E * FT * k + s - 3))
                hi, lo = (w[:, 0, s * 128:(s + 1) * 128] for w in (w_hi, w_lo))
                x_hi, x_lo = (a[:, bass.ds(at(BLOCK * k), BLOCK)] for a in (x2T_hi, x2T_lo))
                pe.matmul(h_ps[s % 4], hi, x_hi, start=True, stop=False)
                pe.matmul(h_ps[s % 4], hi, x_lo, start=False, stop=False)
                pe.matmul(h_ps[s % 4], lo, x_hi, start=False, stop=True).then_inc(s_h, 1)

            def expert_out(k, s):
                e, f = s // FT, s % FT
                pe.wait_ge(s_g_lo, at(E * FT * k + s + 1))
                if f == 0:
                    after(pe, s_weighted, E * k + e - 1)
                hi, lo = (w[:, 1, s * 128:(s + 1) * 128] for w in (w_hi, w_lo))
                pe.matmul(oe_ps[e % 2], hi, g_hi[:, s % 4, :], start=(f == 0), stop=False)
                pe.matmul(oe_ps[e % 2], lo, g_hi[:, s % 4, :], start=False, stop=False)
                pe.matmul(oe_ps[e % 2], hi, g_lo[:, s % 4, :], start=False, stop=(f == FT - 1)).then_inc(s_oe, 1)

            def transpose_gates(k):
                if k == 0:
                    pe.wait_ge(s_gsteps, GATES_MADE)
                after(pe, s_gatesT_sb, k - 1)
                for n in range(TPB):
                    ins = pe.transpose((b2_ps, fin_ps)[k % 2][0:E, n * N:(n + 1) * N], gates[:, TPB * k + n, :], ident[:, :])
                ins.then_inc(s_gatesT, 1)

            def transpose_sum(k):
                pe.wait_ge(s_acc, at(E * (k + 1)))
                for n in range(TPB):
                    ins = pe.transpose(fin_ps[:, n * N:(n + 1) * N], acc[:, n * N:(n + 1) * N], ident[:, :])
                ins.then_inc(s_fin, 1)

            def block_of(k, first):
                for s in range(E * FT):
                    hidden(k, s)
                    if s >= 2:
                        expert_out(k, s - 2)
                    elif not first:
                        expert_out(k - 1, E * FT - 2 + s)
                    if first and s < TPB:
                        transpose_gates(s)
                    if s == 4:
                        pe.wait_ge(s_gatesT_sb, TPB)
                        after(pe, s_acc, E * (k - 1) + 1)
                        pe.matmul(b2_ps, b2_rows[:, :], gatesT[:, bass.ds(at(BLOCK * k), BLOCK)], start=True,
                                  stop=True).then_inc(s_b2, 1)
                    if s == 5 and not first:
                        transpose_sum(k - 1)

            block_of(0, True)
            with pe.Fori(0, NBLOCKS - 1) as k:
                block_of(Count(k, 1, 1), False)
            k = NBLOCKS - 1
            expert_out(k, E * FT - 2)
            expert_out(k, E * FT - 1)
            transpose_sum(k)


CONSTS = 16 * 9
GATE_DIFF = 4
GATES_MADE = 12

_INS = ['x', 'ctx_1024', 'L0_attn_ln_gamma', 'L0_attn_ln_beta', 'L0_attn_w_qkv', 'L0_attn_w_out', 'L0_attn_b_out',
        'L0_ffn_gate_w', 'L0_ffn_gate_b', 'L0_ffn_w1', 'L0_ffn_b1', 'L0_ffn_w2', 'L0_ffn_b2', 'L0_ffn_ln_g',
        'L0_ffn_ln_b']


def shape_constants():
    import numpy as np
    inv = (1.0 / 10000.0 ** (np.arange(0, HD, 2, dtype=np.float32) / np.float32(HD))).astype(np.float32)
    angle = np.arange(N, dtype=np.float32)[:, None] * inv[None, :]
    sin, cos = np.sin(angle), np.cos(angle)
    table = np.stack([np.concatenate([cos, cos], 1), np.concatenate([sin, -sin], 1)], 1)
    rope = np.stack([table * np.float32(HD ** -0.5), table], 1).astype(np.float32)
    masks = np.zeros((3, 128, 128), np.float32)
    masks[0] = np.eye(128)
    masks[1] = np.triu(np.ones((128, 128)), 1) * -1e10
    masks[2] = np.arange(128)[None, :]
    return {"rope": rope, "masks": masks}


def kernel(**inputs):
    import numpy as _np
    import concourse.bacc as _bacc
    from concourse import mybir as _mybir
    from concourse.bass_utils import run_bass_kernel_spmd as _run

    nc = _bacc.Bacc("TRN2", target_bir_lowering=False, num_devices=1)
    arrays, args = {}, []
    given = [(name, _np.ascontiguousarray(inputs[name])) for name in _INS] + list(shape_constants().items())
    for name, a in given:
        arrays[f"in_{name}_dram"] = a
        args.append(nc.dram_tensor(f"in_{name}_dram", a.shape, _mybir.dt.from_np(a.dtype), kind="ExternalInput").ap())
    args.append(nc.dram_tensor("out_0_dram", (B, N, D), F32, kind="ExternalOutput").ap())
    decoder_kernel(nc, *args)
    r = _run(nc, [arrays], core_ids=[0])
    return r.results[0]["out_0_dram"]
```

```python
import math
from contextlib import ExitStack

import concourse.bass as bass
from concourse import mybir

F32 = mybir.dt.float32
F32R = mybir.dt.float32r
U32 = mybir.dt.uint32
ALU = mybir.AluOpType
ACT = mybir.ActivationFunctionType
AX = mybir.AxisListType

B, N, D = 16, 128, 128
H, HD = 16, 64
PAIRS = H // 2
QUADS = H // 4
E, F = 8, 512
FT = F // 128
CHUNK = 512
BLOCK = 512
NBLOCKS = B * N // BLOCK
TPB = BLOCK // N
WCOLS = E * F // B
EPS = 1e-5
INV_TEMP = 1.0 / 0.9
CROSS_SCALE = float(D) ** -0.5

CHUNKS = [0, 2 * CHUNK, CHUNK, 3 * CHUNK, 4 * CHUNK, 5 * CHUNK]
ROPE_CHUNKS = 4
COS, SIN = 0, 1


def head_of(t, j):
    return 4 * (t // 2) + j, t % 2


def made(count, most):
    return min(count, most) if isinstance(count, int) else count


class Count:

    def __init__(self, register, times=1, plus=0):
        self.register, self.times, self.plus = register, times, plus

    def __add__(self, n):
        return Count(self.register, self.times, self.plus + n)

    def __sub__(self, n):
        return self + -n

    def __mul__(self, n):
        return Count(self.register, self.times * n, self.plus * n)

    __radd__, __rmul__ = __add__, __mul__


def at(n):
    if isinstance(n, int):
        return n
    value = n.register * n.times if n.times != 1 else n.register
    return value + n.plus if n.plus else value


class Turn:

    def __init__(self, i, parity):
        self.i, self.parity, self.b = i, parity, 2 * i + parity

    def has(self, k):
        return not isinstance(self.b, int) or 0 <= self.b + k < B

    def ring(self, k):
        return (self.parity + k) % 2


def turns(eng, iteration):
    for b in range(-3, 4):
        iteration(Turn(b // 2, b % 2))
    with eng.Fori(0, B // 2 - 4) as i:
        iteration(Turn(Count(i, 1, 2), 0))
        iteration(Turn(Count(i, 1, 2), 1))
    for b in range(B - 4, B + 3):
        iteration(Turn(b // 2, b % 2))


def drained(b, slot):
    return (b, slot) if isinstance(b, int) and b >= B - 1 else None


def after(eng, sem, count):
    if not isinstance(count, int) or count > 0:
        eng.wait_ge(sem, at(count))


def decoder_kernel(nc, x, ctx_kv, ln_gamma, ln_beta, w_qkv, w_out, b_out, gate_w, gate_b,
                   w1, b1, w2, b2, ffn_g, ffn_b, rope, masks, out):
    with ExitStack() as stack:
        def sb(name, shape, dt=F32):
            return stack.enter_context(nc.sbuf_tensor(name, shape, dt))

        def sem(name):
            return stack.enter_context(nc.semaphore(name))

        gates_dram = nc.dram_tensor("gates_by_expert", (E, B * N), F32, kind="Internal").ap()

        ps = stack.enter_context(nc.psum_tensor("ps", [128, 8, 512], F32))
        proj_ps = [ps[:, 0, :], ps[:, 1, :]]
        turn_ps = ps[:, 2, :]
        score_ps = [ps[:, 3, :], ps[:, 4, :]]
        probsT_ps = ps[:, 5, :]
        pv_ps = ps[:, 6, :]
        small_ps = ps[:, 7, 0:N]
        h_ps = [ps[:, n, :] for n in (0, 1, 3, 6)]
        oe_ps = [ps[:, 4, :], ps[:, 5, :]]
        b2_ps = ps[:, 2, :]
        fin_ps = ps[:, 7, :]
        logits_ps = [h_ps[1], fin_ps]
        gatesT_ps = [oe_ps[1], fin_ps, fin_ps, fin_ps]

        ident = sb("ident", [128, 128])
        cmask = sb("cmask", [128, 128])
        iota8 = sb("iota8", [128, E])
        ropes = sb("ropes", [128, 2, 2, HD])
        vec_rows = sb("vec_rows", [2 + E * FT, 128])
        vec_cols = sb("vec_cols", [128, 2 + E * FT])
        gamma, beta = vec_cols[:, 0:1], vec_cols[:, 1:2]
        bout_bc = sb("bout_bc", [128, D])
        gateb_bc = sb("gateb_bc", [128, E])
        ffng_bc = sb("ffng_bc", [128, D])
        ffnb_bc = sb("ffnb_bc", [128, D])
        gatew = sb("gatew", [128, E])
        b2_rows = sb("b2_rows", [E, D])
        half = sb("half", [128, 1])
        euler = sb("euler", [128, 1])
        hold = sb("hold", [128, 1])
        wqkv_hi = sb("wqkv_hi", [128, 6, CHUNK], F32R)
        wqkv_lo = sb("wqkv_lo", [128, 6, CHUNK], F32R)
        wout = sb("wout", [128, PAIRS, D])
        w_stage = sb("w_stage", [128, 2, 2, WCOLS])
        w_hi = sb("w_hi", [128, 2, E * F], F32R)
        w_lo = sb("w_lo", [128, 2, E * F], F32R)

        x_all = sb("x_all", [128, B, D])
        ctx_in = sb("ctx_in", [128, 2, D])
        xc = sb("xc", [128, 2, D])
        xn_f = sb("xn_f", [128, 2, N])
        xn_hi = sb("xn_hi", [128, 2, N], F32R)
        xn_lo = sb("xn_lo", [128, 2, N], F32R)
        rope_cos = sb("rope_cos", [128, 2, CHUNK])
        rope_sin = sb("rope_sin", [128, 2, CHUNK])
        rot = sb("rot", [128, 2, CHUNK])
        rotT = sb("rotT", [128, 2, 2, PAIRS, N])
        v_sb = sb("v_sb", [128, 2, H * HD])
        probs = sb("probs", [128, QUADS, 4, N])
        negmax = sb("negmax", [128, QUADS, 4])
        den = sb("den", [128, QUADS, 4])
        rden = sb("rden", [128, QUADS, 4])
        probsT = sb("probsT", [128, 2, 4, N])
        headsT = sb("headsT", [128, 2, PAIRS, N])
        y1 = sb("y1", [128, D])
        x1 = sb("x1", [128, 2, D])
        x1ctxT = sb("x1ctxT", [128, 2, N])
        cdots = sb("cdots", [128, N])
        cprobs = sb("cprobs", [128, N])
        cprobsT = sb("cprobsT", [128, N])
        cneg = sb("cneg", [128, 2])
        cden = sb("cden", [128, 2])
        y2 = sb("y2", [128, D])
        x2 = sb("x2", [128, 2, D])
        x2T = sb("x2T", [128, B * N])
        x2T_hi = sb("x2T_hi", [128, B * N], F32R)
        x2T_lo = sb("x2T_lo", [128, B * N], F32R)

        wqkv_in = [x2T[:, c * CHUNK:(c + 1) * CHUNK] for c in range(4)] + [
            v_sb[:, 1, j * CHUNK:(j + 1) * CHUNK] for j in range(2)]

        g_f = [rope_cos[:, n, :] for n in range(2)]
        g_hi = wqkv_hi[:, 0:4, :]
        g_lo = wqkv_lo[:, 0:4, :]
        gates_bc = rotT[:, :, :, :, :].rearrange("p r q a b -> p (r q a b)").rearrange("p (e n) -> p e n", e=E)
        weighted = [probs[:, n, :, :].rearrange("p a b -> p (a b)") for n in range(2)]
        acc = probs[:, 2, :, :].rearrange("p a b -> p (a b)")
        logits = sb("logits", [128, B, E])
        top = sb("top", [128, B, 8])
        top_at = sb("top_at", [128, B, 8], U32)
        top_atf = sb("top_atf", [128, B, 2])
        pair_g = sb("pair_g", [128, 4, B])
        hot = sb("hot", [128, 2, B, E])
        gates = sb("gates", [128, B, E])
        gatesT = headsT[0:E, :, :, :].rearrange("p r a b -> p (r a b)")
        z1 = v_sb[:, 0, 0:BLOCK].rearrange("p (t d) -> p t d", t=TPB)
        z2 = v_sb[:, 0, BLOCK:2 * BLOCK].rearrange("p (t d) -> p t d", t=TPB)
        res = v_sb[:, 1, 0:BLOCK].rearrange("p (t d) -> p t d", t=TPB)

        class Norm:

            def __init__(self, name, tiles=1):
                self.stats = sb(name + "_stats", [128, tiles, 6])
                self.mv = sb(name + "_mv", [128, tiles, 2])
                self.veps = sb(name + "_veps", [128, tiles])
                self.rstd = sb(name + "_rstd", [128, tiles])
                self.s_stats = sem(name + "_stats_made")
                self.s_mv = sem(name + "_moments_made")
                self.s_veps = sem(name + "_veps_made")
                self.s_rstd = sem(name + "_rstd_made")

            def moments(self, dve, tiles, n):
                k = len(tiles)
                for t, tile in enumerate(tiles):
                    dve.bn_stats(self.stats[:, t, :], tile).then_inc(self.s_stats, 1)
                dve.wait_ge(self.s_stats, at(k * n))
                dve.memset(hold[:, :], 0.0)
                for t in range(k):
                    dve.bn_aggr(self.mv[:, t, :], self.stats[:, t, :]).then_inc(self.s_mv, 1)
                dve.wait_ge(self.s_mv, at(k * n))
                dve.tensor_scalar(self.veps[:, 0:k], self.mv[:, :, 1], EPS, None,
                                  ALU.add).then_inc(self.s_veps, 1)

            def root(self, pool, n):
                pool.wait_ge(self.s_veps, at(n))
                k = self.rstd.shape[1]
                pool.tensor_tensor(self.rstd[:, :], self.veps[:, :], half[:, :].to_broadcast([128, k]),
                                   ALU.pow).then_inc(self.s_rstd, 1)

        norm_x, norm_1, norm_2 = Norm("norm_x"), Norm("norm_1"), Norm("norm_2")
        norm_f, norm_3 = Norm("norm_f", TPB), Norm("norm_3", TPB)
        half_f, half_3 = ([Norm(f"half_{which}_{j}", TPB // 2) for j in range(2)] for which in "f3")
        fin_halves = [fin_ps, h_ps[0]]

        s_x = [sem("x_first_loaded"), sem("x_rest_loaded")]
        s_first = sem("ident_and_vectors_loaded")
        s_rope = sem("rope_tables_loaded")
        s_bout = sem("b_out_loaded")
        s_const = sem("other_consts_loaded")
        s_wqkv = [sem(f"wqkv_chunk_{c}_loaded") for c in range(6)]
        s_ctx = [sem("ctx_even_loaded"), sem("ctx_odd_loaded")]
        s_w = [sem("w_even_loaded"), sem("w_odd_loaded")]
        s_turned = sem("three_transposed")
        s_x2T = sem("x2_transposed")
        s_proj = sem("proj_made")
        s_rotT = sem("rot_transposed")
        s_scores = sem("scores_made")
        s_probsT = sem("probs_transposed")
        s_pv = sem("pv_made")
        s_attn = sem("attn_out_made")
        s_dots = sem("cross_dots_made")
        s_cprobsT = sem("cross_probs_transposed")
        s_cross = sem("cross_out_made")
        s_vecT = sem("vec_transposed")
        s_vec = sem("vec_cols_made")
        s_half = sem("half_set")
        s_wqkv_lo = [sem("wqkv_lo_made_by_VectorE"), sem("wqkv_lo_made_by_GpSimd")]
        s_xc = sem("xc_made")
        s_roped = sem("rope_products_made")
        s_negmax = sem("negmax_made")
        s_rden = sem("rden_made")
        s_heads = sem("heads_copied")
        s_y1 = sem("y1_made")
        s_x1 = sem("x1_made")
        s_cdots = sem("cross_dots_masked")
        s_cmax = sem("cross_max_made")
        s_cneg = sem("cross_negmax_made")
        s_crden = sem("cross_rden_made")
        s_y2 = sem("y2_made")
        s_x2 = sem("x2_made")
        s_wqkv_hi = sem("wqkv_hi_made")
        s_xn = sem("xn_made")
        s_rotT_sb = sem("rotT_copied")
        s_v = sem("v_copied")
        s_exp = sem("exp_made")
        s_probsT_sb = sem("probsT_copied")
        s_x1ctxT_sb = sem("x1ctxT_copied")
        s_cexp = sem("cross_exp_made")
        s_cprobsT_sb = sem("cross_probsT_copied")
        s_x2T_sb = sem("x2T_copied")
        s_w_hi = sem("w_hi_made")
        s_rot = sem("rot_made")
        s_probs = sem("probs_normalised")
        s_biased = sem("x_biased")
        s_xn_lo = sem("xn_lo_made")
        s_x2_kept = sem("x2_kept")
        s_x2_lo = sem("x2_lo_made")
        s_w_lo = sem("w_lo_made")
        s_logits = sem("logits_made")
        s_gsteps = sem("gating_steps_done")
        s_gexp = sem("gate_exp_made")
        s_gatesT = sem("gates_transposed")
        s_gatesT_sb = sem("gatesT_copied")
        s_gates_out = sem("gates_stored")
        s_gbc = [sem(f"gates_bc_loaded_{e}") for e in range(E)]
        s_h = sem("hidden_made")
        s_gelu = sem("gelu_made")
        s_g_lo = sem("gelu_lo_made")
        s_oe = sem("expert_out_made")
        s_b2 = sem("b2_part_made")
        s_weighted = sem("expert_weighted")
        s_acc = sem("experts_summed")
        s_fin = sem("moe_transposed")
        s_shifted = sem("residual_shifted")
        s_z = sem("ffn_scaled")
        s_y3 = sem("ffn_residual_added")
        s_res = sem("final_normalised")
        s_out = sem("out_stored")

        block = stack.enter_context(nc.Block())

        def bcast(v):
            return v.rearrange("(a n) -> a n", a=1).to_broadcast([128, v.shape[0]])

        def store(sp, k):
            sp.wait_ge(s_res, at(k + 1))
            sp.dma_start(out[bass.ds(at(TPB * k), TPB)].rearrange("b p d -> p b d"), res).then_inc(s_out, 16)

        @block.sync
        def _(sp):
            sp.sem_inc(s_out, 16)
            x_t = x.rearrange("b p d -> p b d")
            sp.dma_start(x_all[:, 0:2, :], x_t[:, 0:2, :]).then_inc(s_x[0], 16)
            for c, col in enumerate(CHUNKS):
                sp.dma_start(wqkv_in[c], w_qkv[:, col:col + CHUNK]).then_inc(s_wqkv[c], 16)
                if c == 1:
                    sp.dma_start(ropes[:, :, :, :], rope).then_inc(s_rope, 16)
            sp.dma_start(bout_bc[:, :], bcast(b_out)).then_inc(s_bout, 16)
            sp.dma_start(x_all[:, 2:B, :], x_t[:, 2:B, :]).then_inc(s_x[1], 16)
            others = [(wout[:, :, :], w_out.rearrange("(t p) d -> p t d", p=128)),
                      (cmask[:, :], masks[1]), (iota8[:, :], masks[2][:, 0:E]), (gateb_bc[:, :], bcast(gate_b)),
                      (ffng_bc[:, :], bcast(ffn_g)), (ffnb_bc[:, :], bcast(ffn_b)), (gatew[:, :], gate_w),
                      (b2_rows[:, :], b2)]
            assert 16 * len(others) == CONSTS
            for dst, src in others:
                sp.dma_start(dst, src).then_inc(s_const, 16)

            def iteration(t):
                if t.has(0):
                    r, b = t.ring(0), t.b
                    after(sp, s_w_lo, b - 1)
                    sp.dma_start(w_stage[:, r, 0, :],
                                 w1[at(t.i), :, r * WCOLS:(r + 1) * WCOLS]).then_inc(s_w[r], 16)
                    sp.dma_start(w_stage[:, r, 1, :].rearrange("p (f d) -> p f d", d=D),
                                 w2[at(t.i), r * 2 * 128:(r + 1) * 2 * 128, :].rearrange("(f p) d -> p f d", p=128)
                                 ).then_inc(s_w[r], 16)
                if t.has(-1):
                    r = t.ring(-1)
                    after(sp, s_cross, t.b - 2)
                    sp.dma_start(ctx_in[:, r, :], ctx_kv[at(t.b - 1)]).then_inc(s_ctx[r], 16)

            turns(sp, iteration)

            sp.wait_ge(s_gatesT_sb, 1)
            sp.dma_start(gates_dram[:, 0:BLOCK], gatesT[:, 0:BLOCK]).then_inc(s_gates_out, 16)
            sp.wait_ge(s_gates_out, 16)

            def gates_of(k):
                for e in range(E):
                    after(sp, s_weighted, E * (k - 1) + e + 1)
                    sp.dma_start(gates_bc[:, e, :],
                                 gates_dram[e:e + 1, bass.ds(at(BLOCK * k), BLOCK)].to_broadcast([128, BLOCK])
                                 ).then_inc(s_gbc[e], 16)

            gates_of(0)
            sp.wait_ge(s_gatesT_sb, NBLOCKS)
            sp.dma_start(gates_dram[:, BLOCK:B * N], gatesT[:, BLOCK:B * N]).then_inc(s_gates_out, 16)
            sp.wait_ge(s_gates_out, 32)
            with sp.Fori(0, NBLOCKS - 1) as k:
                gates_of(Count(k, 1, 1))
                store(sp, Count(k))
            for j in range(2):
                n = TPB * (NBLOCKS - 1) + HALF * j
                sp.wait_ge(s_res, NBLOCKS + j)
                sp.dma_start(out[n:n + HALF].rearrange("b p d -> p b d"),
                             res[:, HALF * j:HALF * (j + 1), :]).then_inc(s_out, 16)
            sp.wait_ge(s_out, 16 * (NBLOCKS + 2))

        @block.scalar
        def _(act):
            for dst, src in [(ident[:, :], masks[0]), (vec_rows[0:1, :], ln_gamma.rearrange("(a n) -> a n", a=1)),
                             (vec_rows[1:2, :], ln_beta.rearrange("(a n) -> a n", a=1)),
                             (vec_rows[2:2 + E * FT, :], b1.rearrange("e (f p) -> (e f) p", p=128))]:
                act.dma_start(dst, src).then_inc(s_first, 16)

            def wqkv_high(c):
                act.wait_ge(s_wqkv[c], 16)
                act.activation(wqkv_hi[:, c, :], wqkv_in[c], ACT.Copy).then_inc(s_wqkv_hi, 1)

            wqkv_high(0)
            wqkv_high(1)
            act.wait_ge(s_vec, 1)

            def gelu(k, s):
                act.wait_ge(s_h, at(E * FT * k + s + 1))
                after(act, s_g_lo, E * FT * k + s - 1)
                after(act, s_oe, E * FT * k + s - 3)
                b1_col = vec_cols[:, 2 + s:3 + s]
                act.activation(g_f[s % 2], h_ps[s % 4], ACT.Gelu, bias=b1_col).then_inc(s_gelu, 1)
                act.activation(g_hi[:, s % 4, :], h_ps[s % 4], ACT.Gelu, bias=b1_col).then_inc(s_gelu, 1)

            early = {(B, 2): [0, 1], (B + 1, 3): [2], (B + 2, 0): [3, 4], (B + 2, 1): [5], (B + 2, 3): [6, 7]}

            def drain(b, slot):
                for s in early.get(drained(b, slot), []):
                    gelu(0, s)

            def exps(b, t):
                act.wait_ge(s_negmax, at(4 * b + t + 1))
                after(act, s_probsT, 4 * (b - 1) + t + 1)
                for h in range(4):
                    e = act.activation(probs[:, t, h, :], score_ps[t % 2][:, h * N:(h + 1) * N], ACT.Exp,
                                       bias=negmax[:, t, h:h + 1], accum_out=den[:, t, h:h + 1])
                e.then_inc(s_exp, 1)

            def probsT_copy(b, t):
                act.wait_ge(s_probsT, at(4 * b + t + 1))
                after(act, s_pv, 2 * b + t // 2)
                act.activation(probsT[:, t % 2, :, :].rearrange("p a b -> p (a b)"), probsT_ps,
                               ACT.Copy).then_inc(s_probsT_sb, 1)

            def rotT_copy(b, r, c):
                act.wait_ge(s_rotT, at(4 * b + c + 1))
                act.activation(rotT[:, r, c % 2, 4 * (c // 2):4 * (c // 2) + 4, :],
                               turn_ps.rearrange("p (a b) -> p a b", a=4), ACT.Copy).then_inc(s_rotT_sb, 1)

            def iteration(t):
                b = t.b
                if t.has(-1):
                    probsT_copy(b - 1, 2)
                if t.has(0):
                    rotT_copy(b, t.ring(0), 2)
                    exps(b, 0)
                if t.has(-2) or t.has(2):
                    act.wait_ge(s_turned, at(b + 3))
                if t.has(-2):
                    act.activation(x1ctxT[:, :, :].rearrange("p a b -> p (a b)"), turn_ps[:, 0:2 * N],
                                   ACT.Copy).then_inc(s_x1ctxT_sb, 1)
                if t.has(2):
                    after(act, s_proj, 6 * (b + 1))
                    for xn in (xn_f, xn_hi):
                        act.activation(xn[:, t.ring(2), :], turn_ps[:, 2 * N:3 * N], ACT.Identity, bias=beta,
                                       scale=gamma).then_inc(s_xn, 1)
                drain(b, 0)
                if isinstance(b, int) and b == -2:
                    for c in range(2, 6):
                        wqkv_high(c)
                if t.has(-1):
                    probsT_copy(b - 1, 3)
                if t.has(0):
                    rotT_copy(b, t.ring(0), 3)
                    exps(b, 1)
                drain(b, 1)
                if t.has(0):
                    probsT_copy(b, 0)
                if t.has(1):
                    rotT_copy(b + 1, t.ring(1), 0)
                if t.has(0):
                    exps(b, 2)
                if t.has(-2):
                    act.wait_ge(s_cneg, at(b - 1))
                    act.activation(cprobs[:, :], cdots[:, :], ACT.Exp, bias=cneg[:, 1:2], scale=CROSS_SCALE,
                                   accum_out=cden[:, 0:1]).then_inc(s_cexp, 1)
                drain(b, 2)
                if t.has(-3):
                    act.wait_ge(s_x2T, at(b - 2))
                    for x2_turned in (x2T, x2T_hi):
                        act.activation(x2_turned[:, bass.ds(at((b - 3) * N), N)], turn_ps[:, 0:N],
                                       ACT.Copy).then_inc(s_x2T_sb, 1)
                drain(b, 3)
                if t.has(0):
                    probsT_copy(b, 1)
                if t.has(1):
                    rotT_copy(b + 1, t.ring(1), 1)
                if t.has(0):
                    exps(b, 3)
                if t.has(-2):
                    act.wait_ge(s_cprobsT, at(b - 1))
                    act.activation(cprobsT[:, :], turn_ps[:, 0:N], ACT.Copy).then_inc(s_cprobsT_sb, 1)
                if t.has(1):
                    after(act, s_pv, 2 * b)
                    for j in range(2):
                        act.wait_ge(s_proj, at(6 * (b + 1) + 5 + j))
                        act.activation(v_sb[:, t.ring(1), j * CHUNK:(j + 1) * CHUNK], proj_ps[j],
                                       ACT.Copy).then_inc(s_v, 1)
                if t.has(0):
                    act.wait_ge(s_w[t.ring(0)], at(32 * (t.i + 1)))
                    act.activation(w_hi[:, :, bass.ds(at(b * WCOLS), WCOLS)], w_stage[:, t.ring(0), :, :],
                                   ACT.Copy).then_inc(s_w_hi, 1)

            turns(act, iteration)

            for s in range(sum(len(steps) for steps in early.values()), E * FT):
                gelu(0, s)
            with act.Fori(0, NBLOCKS - 1) as k:
                for s in range(E * FT):
                    gelu(Count(k, 1, 1), s)

        @block.gpsimd
        def _(pool):
            pool.wait_ge(s_half, 1)

            def wqkv_low(c):
                pool.wait_ge(s_wqkv_hi, c + 1)
                pool.tensor_tensor(wqkv_lo[:, c, :], wqkv_in[c], wqkv_hi[:, c, :],
                                   ALU.subtract).then_inc(s_wqkv_lo[1], 1)

            def gate_exp(part):
                pool.wait_ge(s_gsteps, GATE_STEPS * part + GATE_DIFF)
                n0, n1 = ROUTED[part]
                pool.tensor_tensor(pair_g[:, 1, n0:n1], euler[:, :].to_broadcast([128, n1 - n0]), pair_g[:, 0, n0:n1],
                                   ALU.pow).then_inc(s_gexp, 1)

            def rotate(b, c):
                pool.wait_ge(s_roped, at(4 * b + c + 1))
                after(pool, s_rotT, 4 * b + c - 1)
                o = rot[:, c % 2, :].rearrange("p (h s j) -> p h s j", s=2, j=HD // 2)
                co = rope_cos[:, c % 2, :].rearrange("p (h s j) -> p h s j", s=2, j=HD // 2)
                si = rope_sin[:, c % 2, :].rearrange("p (h s j) -> p h s j", s=2, j=HD // 2)
                pool.tensor_tensor(o[:, :, 0, :], co[:, :, 0, :], si[:, :, 1, :], ALU.add)
                pool.tensor_tensor(o[:, :, 1, :], co[:, :, 1, :], si[:, :, 0, :], ALU.add).then_inc(s_rot, 1)

            def normalise(b, t):
                pool.wait_ge(s_rden, at(4 * b + t + 1))
                pool.tensor_tensor(probs[:, t, :, :], probs[:, t, :, :],
                                   rden[:, t, :].unsqueeze(2).to_broadcast([128, 4, N]),
                                   ALU.mult).then_inc(s_probs, 1)

            def iteration(t):
                b = t.b
                if t.has(-1):
                    normalise(b - 1, 3)
                if t.has(-3):
                    norm_2.root(pool, b - 2)
                if t.has(1):
                    rotate(b + 1, 0)
                if t.has(0):
                    normalise(b, 0)
                if t.has(1):
                    rotate(b + 1, 1)
                if drained(b, 0) == (B + 1, 0):
                    gate_exp(0)
                if isinstance(b, int) and b == -1:
                    for c in POOL_LOWS[1:]:
                        wqkv_low(c)
                if t.has(2):
                    pool.wait_ge(s_xn, at(2 * (b + 3)))
                    pool.tensor_tensor(xn_lo[:, t.ring(2), :], xn_f[:, t.ring(2), :], xn_hi[:, t.ring(2), :],
                                       ALU.subtract).then_inc(s_xn_lo, 1)
                if t.has(-3):
                    pool.wait_ge(s_x2, at(b - 2))
                    pool.tensor_copy(x_all[:, bass.ds(at(b - 3), 1), :], x2[:, t.ring(-3), :].unsqueeze(1)).then_inc(s_x2_kept, 1)
                if t.has(0):
                    normalise(b, 1)
                if t.has(3):
                    norm_x.root(pool, b + 4)
                if isinstance(b, int) and b == -2:
                    wqkv_low(POOL_LOWS[0])
                if t.has(1):
                    rotate(b + 1, 2)
                if t.has(-1):
                    norm_1.root(pool, b)
                if t.has(-1):
                    pool.wait_ge(s_w_hi, at(b))
                    cols = bass.ds(at((b - 1) * WCOLS), WCOLS)
                    pool.tensor_tensor(w_lo[:, :, cols], w_stage[:, t.ring(-1), :, :], w_hi[:, :, cols],
                                       ALU.subtract).then_inc(s_w_lo, 1)
                if t.has(0):
                    normalise(b, 2)
                if t.has(-3):
                    pool.wait_ge(s_x2T_sb, at(2 * (b - 2)))
                    pool.tensor_tensor(x2T_lo[:, bass.ds(at((b - 3) * N), N)], x2T[:, bass.ds(at((b - 3) * N), N)],
                                       x2T_hi[:, bass.ds(at((b - 3) * N), N)], ALU.subtract).then_inc(s_x2_lo, 1)
                if t.has(1):
                    rotate(b + 1, 3)
                if t.has(2):
                    if isinstance(b, int) and b == -2:
                        pool.wait_ge(s_bout, 16)
                    pool.wait_ge(s_xc, at(b + 3))
                    pool.tensor_tensor(x_all[:, bass.ds(at(b + 2), 1), :], x_all[:, bass.ds(at(b + 2), 1), :],
                                       bout_bc[:, :].unsqueeze(1), ALU.add).then_inc(s_biased, 1)

            turns(pool, iteration)

            def sum_expert(k, e):
                pool.wait_ge(s_weighted, at(E * k + e + 1))
                pool.wait_ge(s_acc, at(E * k + e))
                pool.tensor_tensor(acc, acc, weighted[e % 2], ALU.add).then_inc(s_acc, 1)

            pool.wait_ge(s_x2_kept, B)
            for k in range(NBLOCKS):
                pool.tensor_tensor(x_all[:, TPB * k:TPB * (k + 1), :], x_all[:, TPB * k:TPB * (k + 1), :],
                                   ffnb_bc[:, :].unsqueeze(1).to_broadcast([128, TPB, D]), ALU.add).then_inc(s_shifted, 1)
            for e in range(1, E):
                sum_expert(0, e)
                if e == 2:
                    gate_exp(1)

            def block_of(k, last):
                for e in range(1, E - 1 if last else E):
                    if e == 1:
                        norm_f.root(pool, k)
                    if e == 3:
                        norm_3.root(pool, k)
                    sum_expert(k, e)

            with pool.Fori(0, NBLOCKS - 2) as i:
                block_of(Count(i, 1, 1), False)
            block_of(NBLOCKS - 1, True)
            for norm in half_f + half_3:
                norm.root(pool, 1)

        @block.vector
        def _(dve):
            dve.memset(euler[:, :], math.e)
            dve.memset(half[:, :], -0.5).then_inc(s_half, 1)

            def rope_products(b, c):
                dve.wait_ge(s_proj, at(6 * b + c + 1))
                after(dve, s_rot, 4 * b + c - 1)
                p = proj_ps[c % 2].rearrange("p (h j) -> p h j", j=HD)
                for kind, dst in ((COS, rope_cos), (SIN, rope_sin)):
                    table = ropes[:, c % 2, kind, :].unsqueeze(1).to_broadcast([128, CHUNK // HD, HD])
                    ins = dve.tensor_tensor(dst[:, c % 2, :].rearrange("p (h j) -> p h j", j=HD), p, table, ALU.mult)
                ins.then_inc(s_roped, 1)

            def row_max(b, t):
                dve.wait_ge(s_scores, at(4 * b + t + 1))
                dve.tensor_reduce(negmax[:, t, :], score_ps[t % 2].rearrange("p (h k) -> p h k", h=4), AX.X,
                                  ALU.max, negate=True).then_inc(s_negmax, 1)

            def recip(b, t):
                dve.wait_ge(s_exp, at(4 * b + t + 1))
                dve.reciprocal(rden[:, t, :], den[:, t, :]).then_inc(s_rden, 1)

            def heads_copy(b, r, o):
                dve.wait_ge(s_pv, at(2 * b + o + 1))
                dve.tensor_copy(headsT[:, r, 4 * o:4 * o + 4, :].rearrange("p a b -> p (a b)"),
                                pv_ps).then_inc(s_heads, 1)

            def normed(norm, n, dst, src):
                dve.wait_ge(norm.s_rstd, at(n))
                return dve.tensor_scalar(dst, src, norm.mv[:, 0, 0:1], norm.rstd[:, 0:1], ALU.subtract, ALU.mult)

            def gate_step(n, ins):
                ins.then_inc(s_gsteps, 1)
                dve.wait_ge(s_gsteps, n)

            def two_largest(part):
                n, (n0, n1) = GATE_STEPS * part, ROUTED[part]
                dve.wait_ge(s_logits, part + 1)
                lg = logits[:, n0:n1, :]
                gate_step(n + 1, dve.tensor_tensor(lg, logits_ps[part][:, n0 * E:n1 * E].rearrange("p (t e) -> p t e", e=E),
                                                   gateb_bc[:, :].unsqueeze(1).to_broadcast([128, n1 - n0, E]), ALU.add))
                gate_step(n + 2, dve.tensor_scalar(lg, lg, INV_TEMP, None, ALU.mult))
                for t in range(n0, n1):
                    ins = dve.max(top[:, t, :], logits[:, t, :])
                gate_step(n + 3, ins)

            def largest_experts(part):
                n, (n0, n1) = GATE_STEPS * part, ROUTED[part]
                gate_step(n + 4, dve.tensor_tensor(pair_g[:, 0, n0:n1], top[:, n0:n1, 1], top[:, n0:n1, 0], ALU.subtract))
                for t in range(n0, n1):
                    ins = dve.max_index(top_at[:, t, :], top[:, t, :], logits[:, t, :])
                gate_step(n + 5, ins)
                gate_step(n + 6, dve.tensor_copy(top_atf[:, n0:n1, :], top_at[:, n0:n1, 0:2]))

            def gate_pair(part):
                n, (n0, n1) = GATE_STEPS * part, ROUTED[part]
                dve.wait_ge(s_gexp, part + 1)
                d, e, g0, g1 = (pair_g[:, j, n0:n1] for j in range(4))
                gate_step(n + 7, dve.tensor_scalar(d, e, 1.0, None, ALU.add))
                gate_step(n + 8, dve.reciprocal(g0, d))
                gate_step(n + 9, dve.tensor_tensor(g1, e, g0, ALU.mult))

            def gates_of(part):
                n, (n0, n1) = GATE_STEPS * part, ROUTED[part]
                full = [128, n1 - n0, E]
                for j in range(2):
                    ins = dve.tensor_tensor(hot[:, j, n0:n1, :], iota8[:, :].unsqueeze(1).to_broadcast(full),
                                            top_atf[:, n0:n1, j:j + 1].to_broadcast(full), ALU.is_equal)
                gate_step(n + 10, ins)
                for j in range(2):
                    ins = dve.tensor_tensor(hot[:, j, n0:n1, :], hot[:, j, n0:n1, :],
                                            pair_g[:, 2 + j, n0:n1].unsqueeze(2).to_broadcast(full), ALU.mult)
                gate_step(n + 11, ins)
                gate_step(n + 12, dve.tensor_tensor(gates[:, n0:n1, :], hot[:, 0, n0:n1, :], hot[:, 1, n0:n1, :], ALU.add))

            def gates_copy(k):
                dve.wait_ge(s_gatesT, at(k + 1))
                dve.tensor_copy(gatesT[:, k * BLOCK:(k + 1) * BLOCK], gatesT_ps[k][0:E, :]).then_inc(s_gatesT_sb, 1)

            def gelu_low(k, s):
                dve.wait_ge(s_gelu, at(2 * (E * FT * k + s) + 2))
                after(dve, s_oe, E * FT * k + s - 3)
                dve.tensor_tensor(g_lo[:, s % 4, :], g_f[s % 2], g_hi[:, s % 4, :],
                                  ALU.subtract).then_inc(s_g_lo, 1)

            early = {(B, 3): [0], (B + 1, 0): [1], (B + 1, 3): [2], (B + 2, 0): [3], (B + 2, 1): [4], (B + 2, 2): [5],
                     (B + 2, 3): [6]}

            def drain(b, slot):
                here = drained(b, slot)
                if here == (B, 0):
                    two_largest(0)
                if here == (B, 3):
                    largest_experts(0)
                if here == (B + 1, 1):
                    gate_pair(0)
                    gates_of(0)
                if here == (B + 1, 3):
                    gates_copy(0)
                for s in early.get(here, []):
                    gelu_low(0, s)

            def wqkv_low(c):
                dve.wait_ge(s_wqkv_hi, c + 1)
                dve.tensor_tensor(wqkv_lo[:, c, :], wqkv_in[c], wqkv_hi[:, c, :],
                                  ALU.subtract).then_inc(s_wqkv_lo[0], 1)

            def iteration(t):
                b = t.b
                if t.has(0):
                    row_max(b, 0)
                if t.has(-1):
                    heads_copy(b - 1, t.ring(-1), 0)
                if t.has(-3):
                    dve.wait_ge(s_cross, at(b - 2))
                    dve.wait_ge(s_crden, at(b - 2))
                    dve.scalar_tensor_tensor(y2[:, :], small_ps, cden[:, 1:2], x1[:, t.ring(-3), :], ALU.mult,
                                             ALU.add).then_inc(s_y2, 1)
                    dve.wait_ge(s_y2, at(b - 2))
                    norm_2.moments(dve, [y2[:, :]], b - 2)
                if t.has(1):
                    rope_products(b + 1, 0)
                if t.has(0):
                    recip(b, 0)
                drain(b, 0)
                if t.has(0):
                    row_max(b, 1)
                if t.has(-3):
                    normed(norm_2, b - 2, x2[:, t.ring(-3), :], y2[:, :]).then_inc(s_x2, 1)
                if t.has(1):
                    rope_products(b + 1, 1)
                if t.has(0):
                    recip(b, 1)
                if t.has(-2):
                    dve.wait_ge(s_dots, at(b - 1))
                    dve.tensor_tensor(cdots[:, :], small_ps, cmask[:, :], ALU.add).then_inc(s_cdots, 1)
                    dve.wait_ge(s_cdots, at(b - 1))
                    dve.tensor_reduce(cneg[:, 0:1], cdots[:, :], AX.X, ALU.max, negate=True).then_inc(s_cmax, 1)
                    dve.wait_ge(s_cmax, at(b - 1))
                    dve.tensor_scalar(cneg[:, 1:2], cneg[:, 0:1], CROSS_SCALE, None, ALU.mult).then_inc(s_cneg, 1)
                drain(b, 1)
                if t.has(0):
                    row_max(b, 2)
                if t.has(-1):
                    heads_copy(b - 1, t.ring(-1), 1)
                if t.has(1):
                    rope_products(b + 1, 2)
                if t.has(3):
                    if isinstance(b, int):
                        dve.wait_ge(s_x[0 if b + 3 < 2 else 1], 16)
                    norm_x.moments(dve, [x_all[:, bass.ds(at(b + 3), 1), :].rearrange("p a d -> p (a d)")], b + 4)
                if t.has(0):
                    recip(b, 2)
                if t.has(1):
                    rope_products(b + 1, 3)
                if t.has(-1):
                    dve.wait_ge(s_attn, at(b))
                    dve.wait_ge(s_biased, at(b))
                    dve.tensor_tensor(y1[:, :], small_ps, x_all[:, bass.ds(at(b - 1), 1), :].rearrange("p a d -> p (a d)"),
                                      ALU.add).then_inc(s_y1, 1)
                    dve.wait_ge(s_y1, at(b))
                    norm_1.moments(dve, [y1[:, :]], b)
                drain(b, 2)
                if t.has(0):
                    row_max(b, 3)
                if t.has(3):
                    after(dve, s_turned, b + 2)
                    normed(norm_x, b + 4, xc[:, t.ring(3), :],
                           x_all[:, bass.ds(at(b + 3), 1), :].rearrange("p a d -> p (a d)")).then_inc(s_xc, 1)
                if t.has(-1):
                    normed(norm_1, b, x1[:, t.ring(-1), :], y1[:, :]).then_inc(s_x1, 1)
                if t.has(-2):
                    dve.wait_ge(s_cexp, at(b - 1))
                    dve.reciprocal(cden[:, 1:2], cden[:, 0:1]).then_inc(s_crden, 1)
                if t.has(0):
                    recip(b, 3)
                drain(b, 3)
                if isinstance(b, int) and b == -3:
                    dve.wait_ge(s_vecT, 1)
                    dve.tensor_copy(vec_cols[:, :], probsT_ps[:, 0:2 + E * FT]).then_inc(s_vec, 1)
                    wqkv_low(VECTOR_LOWS[0])
                if isinstance(b, int) and b == -2:
                    for c in VECTOR_LOWS[1:]:
                        wqkv_low(c)
                    dve.wait_ge(s_rope, 16)
                if isinstance(b, int) and b == 0:
                    dve.wait_ge(s_const, CONSTS)

            turns(dve, iteration)

            def weigh(k, e):
                dve.wait_ge(s_oe, at(E * FT * k + FT * (e + 1)))
                dve.wait_ge(s_gbc[e], at(16 * (k + 1)))
                after(dve, s_acc, E * k + e - 1)
                dve.tensor_tensor(weighted[e % 2], oe_ps[e % 2], gates_bc[:, e, :], ALU.mult).then_inc(s_weighted, 1)
                if e == 0:
                    dve.wait_ge(s_weighted, at(E * k + 1))
                    dve.wait_ge(s_b2, at(k + 1))
                    after(dve, s_fin, k)
                    dve.tensor_tensor(acc, weighted[0], b2_ps, ALU.add).then_inc(s_acc, 1)

            def finish_stats(n, norm, m, tiles, fin):
                dve.wait_ge(s_fin, at(n))
                norm.moments(dve, [fin[:, t * N:(t + 1) * N] for t in range(len(tiles))], m)

            def finish_scale(norm, tiles, fin):
                for t, tile in enumerate(tiles):
                    ins = dve.scalar_tensor_tensor(z1[:, tile, :], fin[:, t * N:(t + 1) * N], norm.mv[:, t, 0:1],
                                                   ffng_bc[:, :], ALU.subtract, ALU.mult)
                ins.then_inc(s_z, 1)

            def finish_residual(k, n, norm, m, tiles):
                dve.wait_ge(norm.s_rstd, at(m))
                dve.wait_ge(s_z, at(n))
                for t, tile in enumerate(tiles):
                    ins = dve.scalar_tensor_tensor(z2[:, tile, :], z1[:, tile, :], norm.rstd[:, t:t + 1],
                                                   x_all[:, bass.ds(at(TPB * k + tile), 1), :].rearrange("p a d -> p (a d)"),
                                                   ALU.mult, ALU.add)
                ins.then_inc(s_y3, 1)

            def finish_stats2(n, norm, m, tiles):
                dve.wait_ge(s_y3, at(n))
                norm.moments(dve, [z2[:, tile, :] for tile in tiles], m)

            def finish_norm2(k, norm, m, tiles):
                dve.wait_ge(norm.s_rstd, at(m))
                dve.wait_ge(s_out, at(16 * (k + 1)))
                for t, tile in enumerate(tiles):
                    ins = dve.tensor_scalar(res[:, tile, :], z2[:, tile, :], norm.mv[:, t, 0:1],
                                            norm.rstd[:, t:t + 1], ALU.subtract, ALU.mult)
                ins.then_inc(s_res, 1)

            def step(k, s):
                gelu_low(k, s)
                if s % FT == 2 and s > FT:
                    weigh(k, s // FT - 1)

            for s in range(sum(len(steps) for steps in early.values()), E * FT):
                step(0, s)
                if s == 8:
                    weigh(0, 0)
                if s == 9:
                    gates_copy(1)
                if s == 12:
                    gates_copy(2)
                if s == 15:
                    two_largest(1)
                if s == 17:
                    largest_experts(1)
                if s == 20:
                    gate_pair(1)
                if s == 21:
                    gates_of(1)
                if s == 25:
                    gates_copy(NBLOCKS - 1)
            dve.wait_ge(s_shifted, NBLOCKS)
            with dve.Fori(0, NBLOCKS - 1) as i:
                k = Count(i, 1, 1)
                for s in range(E * FT):
                    step(k, s)
                    if s == 2:
                        weigh(k - 1, E - 1)
                    if s == 9:
                        finish_stats(k, norm_f, k, range(TPB), fin_ps)
                    if s == 12:
                        finish_scale(norm_f, range(TPB), fin_ps)
                    if s == 15:
                        finish_residual(k - 1, k, norm_f, k, range(TPB))
                    if s == 17:
                        finish_stats2(k, norm_3, k, range(TPB))
                    if s == 21:
                        finish_norm2(k - 1, norm_3, k, range(TPB))
            k = NBLOCKS - 1
            weigh(k, E - 1)
            dve.wait_ge(s_weighted, E * (k + 1))
            dve.wait_ge(s_acc, E * k + E - 1)
            for j in range(2):
                cols = slice(HALF * N * j, HALF * N * (j + 1))
                dve.tensor_tensor(acc[:, cols], acc[:, cols], weighted[(E - 1) % 2][:, cols], ALU.add).then_inc(s_acc, 1)
            tiles = [range(HALF * j, HALF * (j + 1)) for j in range(2)]
            for j in range(2):
                finish_stats(NBLOCKS + j, half_f[j], 1, tiles[j], fin_halves[j])
                finish_scale(half_f[j], tiles[j], fin_halves[j])
            for j in range(2):
                finish_residual(k, NBLOCKS + j, half_f[j], 1, tiles[j])
                finish_stats2(NBLOCKS + j, half_3[j], 1, tiles[j])
            for j in range(2):
                finish_norm2(k, half_3[j], 1, tiles[j])

        @block.tensor
        def _(pe):
            pe.wait_ge(s_first, 16 * 4)
            pe.transpose(probsT_ps[:, 0:2 + E * FT], vec_rows[:, :], ident[0:2 + E * FT, 0:2 + E * FT]).then_inc(s_vecT, 1)

            def project(b, r, c):
                if c == 0:
                    pe.wait_ge(s_xn_lo, at(b + 1))
                if c < 2:
                    after(pe, s_v, 2 * b + c - 1)
                else:
                    pe.wait_ge(s_roped, at(4 * b + c - 1))
                if isinstance(b, int) and b == 0:
                    engine = 0 if c in VECTOR_LOWS else 1
                    pe.wait_ge(s_wqkv_lo[engine], (VECTOR_LOWS, POOL_LOWS)[engine].index(c) + 1)
                pe.matmul(proj_ps[c % 2], xn_hi[:, r, :], wqkv_hi[:, c, :], start=True, stop=False)
                pe.matmul(proj_ps[c % 2], xn_hi[:, r, :], wqkv_lo[:, c, :], start=False, stop=False)
                pe.matmul(proj_ps[c % 2], xn_lo[:, r, :], wqkv_hi[:, c, :], start=False,
                          stop=True).then_inc(s_proj, 1)

            def turned_copied(b):
                after(pe, s_x1ctxT_sb, made(b - 1, B))
                after(pe, s_xn, made(2 * (b + 3), 2 * B))

            def transpose_rot(b, c):
                pe.wait_ge(s_rot, at(4 * b + c + 1))
                after(pe, s_rotT_sb, 4 * b + c)
                if c == 0 and isinstance(b, int):
                    turned_copied(b - 1)
                if c == 1:
                    after(pe, s_x2T_sb, 2 * (b - 3))
                if c == 2:
                    after(pe, s_cprobsT_sb, b - 2)
                if c == 3:
                    turned_copied(b)
                for p in range(4):
                    ins = pe.transpose(turn_ps[:, p * N:(p + 1) * N], rot[:, c % 2, p * 128:(p + 1) * 128], ident[:, :])
                ins.then_inc(s_rotT, 1)

            def turn_three(t):
                b = t.b
                after(pe, s_rotT_sb, made(4 * b + 3, 4 * B))
                if isinstance(b, int):
                    after(pe, s_cprobsT_sb, made(b - 2, B))
                    turned_copied(b - 1)
                if t.has(-2):
                    pe.wait_ge(s_x1, at(b - 1))
                    pe.wait_ge(s_ctx[t.ring(-2)], at(16 * t.i))
                    pe.transpose(turn_ps[:, 0:N], x1[:, t.ring(-2), :], ident[:, :])
                    ins = pe.transpose(turn_ps[:, N:2 * N], ctx_in[:, t.ring(-2), :], ident[:, :])
                if t.has(2):
                    pe.wait_ge(s_xc, at(b + 3))
                    ins = pe.transpose(turn_ps[:, 2 * N:3 * N], xc[:, t.ring(2), :], ident[:, :])
                ins.then_inc(s_turned, 1)

            def scores(b, r, t):
                pe.wait_ge(s_rotT_sb, at(4 * b + (2 if t < 2 else 4)))
                after(pe, s_exp, 4 * b + t - 1)
                for j in range(4):
                    pair, side = head_of(t, j)
                    rows = slice(HD * side, HD * side + HD)
                    ins = pe.matmul(score_ps[t % 2][:, j * N:(j + 1) * N], rotT[rows, r, 0, pair, :],
                                    rotT[rows, r, 1, pair, :], start=True, stop=True)
                ins.then_inc(s_scores, 1)

            def transpose_probs(b, t):
                pe.wait_ge(s_probs, at(4 * b + t + 1))
                after(pe, s_probsT_sb, 4 * b + t)
                for j in range(4):
                    ins = pe.transpose(probsT_ps[:, j * N:(j + 1) * N], probs[:, t, j, :], ident[:, :])
                ins.then_inc(s_probsT, 1)

            def values(b, r, o):
                pe.wait_ge(s_probsT_sb, at(4 * b + 2 * o + 2))
                pe.wait_ge(s_v, at(2 * b + 2))
                after(pe, s_heads, 2 * b + o)
                for j in range(8):
                    quad = 2 * o + j % 2
                    pair, side = head_of(quad, j // 2)
                    h = 2 * pair + side
                    ins = pe.matmul(pv_ps[HD * side:HD * side + HD, (j // 2) * N:(j // 2 + 1) * N],
                                    v_sb[:, r, h * HD:(h + 1) * HD], probsT[:, quad % 2, j // 2, :],
                                    start=True, stop=True)
                ins.then_inc(s_pv, 1)

            def hidden(k, s):
                e, f = s // FT, s % FT
                after(pe, s_gelu, 2 * (E * FT * k + s - 3))
                hi, lo = (w[:, 0, s * 128:(s + 1) * 128] for w in (w_hi, w_lo))
                x_hi, x_lo = (a[:, bass.ds(at(BLOCK * k), BLOCK)] for a in (x2T_hi, x2T_lo))
                pe.matmul(h_ps[s % 4], hi, x_hi, start=True, stop=False)
                pe.matmul(h_ps[s % 4], hi, x_lo, start=False, stop=False)
                pe.matmul(h_ps[s % 4], lo, x_hi, start=False, stop=True).then_inc(s_h, 1)

            def expert_out(k, s):
                e, f = s // FT, s % FT
                pe.wait_ge(s_g_lo, at(E * FT * k + s + 1))
                if f == 0:
                    after(pe, s_weighted, E * k + e - 1)
                    if isinstance(k, int) and k == 0 and e == 0:
                        pe.wait_ge(s_exp, 4 * B)
                    if isinstance(k, int) and k == 0 and e == 1:
                        pe.wait_ge(s_gatesT_sb, 1)
                hi, lo = (w[:, 1, s * 128:(s + 1) * 128] for w in (w_hi, w_lo))
                pe.matmul(oe_ps[e % 2], hi, g_hi[:, s % 4, :], start=(f == 0), stop=False)
                pe.matmul(oe_ps[e % 2], lo, g_hi[:, s % 4, :], start=False, stop=False)
                pe.matmul(oe_ps[e % 2], hi, g_lo[:, s % 4, :], start=False, stop=(f == FT - 1)).then_inc(s_oe, 1)

            def step(k, s):
                hidden(k, s)
                if s >= LAG:
                    expert_out(k, s - LAG)
                elif not isinstance(k, int):
                    expert_out(k - 1, E * FT - LAG + s)

            def router(part, n0, n1):
                pe.wait_ge(s_x2T_sb, 2 * n1)
                for n in range(n0, n1):
                    ins = pe.matmul(logits_ps[part][:, n * E:(n + 1) * E], x2T[:, n * N:(n + 1) * N], gatew[:, :],
                                    start=True, stop=True)
                if n1 == ROUTED[part][1]:
                    ins.then_inc(s_logits, 1)

            def transpose_gates(k):
                pe.wait_ge(s_gsteps, GATE_STEPS * (1 if TPB * k < ROUTED[0][1] else 2))
                after(pe, s_gatesT_sb, k)
                for n in range(TPB):
                    ins = pe.transpose(gatesT_ps[k][0:E, n * N:(n + 1) * N], gates[:, TPB * k + n, :], ident[:, :])
                ins.then_inc(s_gatesT, 1)

            early_h = {(B, 1): [0, 1], (B, 2): [2], (B + 1, 0): [3], (B + 1, 1): [4], (B + 1, 2): [5], (B + 2, 0): [6],
                       (B + 2, 1): [7], (B + 2, 3): [8]}
            early_oe = {(B + 1, 1): [0], (B + 1, 2): [1], (B + 2, 0): [2], (B + 2, 1): [3], (B + 2, 3): [4, 5]}

            def drain(b, slot):
                here = drained(b, slot)
                if here == (B - 1, 0):
                    pe.wait_ge(s_v, 2 * B)
                if here is not None and b == B - 1 and slot > 0:
                    router(0, TPB * (slot - 1), TPB * slot)
                if here == (B, 1):
                    pe.wait_ge(s_x2_lo, TPB)
                    pe.wait_ge(s_w_lo, B // 2)
                    pe.wait_ge(s_gsteps, 1)
                if here == (B + 1, 3):
                    pe.wait_ge(s_probsT_sb, 4 * B)
                    transpose_gates(0)
                for s in early_h.get(here, []):
                    hidden(0, s)
                for s in early_oe.get(here, []):
                    expert_out(0, s)

            def iteration(t):
                b = t.b
                if t.has(0):
                    scores(b, t.ring(0), 0)
                if t.has(-1):
                    values(b - 1, t.ring(-1), 0)
                    transpose_probs(b - 1, 2)
                if t.has(0):
                    transpose_rot(b, 2)
                if t.has(-3):
                    pe.wait_ge(s_cprobsT_sb, at(b - 2))
                    after(pe, s_y1, made(b - 1, B))
                    pe.matmul(small_ps, cprobsT[:, :], ctx_in[:, t.ring(-3), :], start=True, stop=True).then_inc(s_cross, 1)
                if t.has(1):
                    project(b + 1, t.ring(1), 0)
                    project(b + 1, t.ring(1), 1)
                if t.has(-2) or t.has(2):
                    turn_three(t)
                drain(b, 0)
                if t.has(0):
                    scores(b, t.ring(0), 1)
                if t.has(-1):
                    transpose_probs(b - 1, 3)
                if t.has(0):
                    transpose_rot(b, 3)
                if t.has(-2):
                    pe.wait_ge(s_x1ctxT_sb, at(b - 1))
                    after(pe, s_y2, b - 2)
                    pe.matmul(small_ps, x1ctxT[:, 0, :], x1ctxT[:, 1, :], start=True, stop=True).then_inc(s_dots, 1)
                if t.has(1):
                    project(b + 1, t.ring(1), 2)
                if isinstance(b, int) and b < B:
                    drain(b, 1)
                if t.has(0):
                    scores(b, t.ring(0), 2)
                if t.has(-1):
                    values(b - 1, t.ring(-1), 1)
                if isinstance(b, int) and b >= B:
                    drain(b, 1)
                if t.has(0):
                    transpose_probs(b, 0)
                if t.has(1):
                    transpose_rot(b + 1, 0)
                    project(b + 1, t.ring(1), 3)
                if t.has(-1):
                    pe.wait_ge(s_heads, at(2 * b))
                    after(pe, s_cdots, b - 1)
                    if isinstance(b, int) and b == 1:
                        pe.wait_ge(s_const, CONSTS)
                    for p in range(PAIRS):
                        ins = pe.matmul(small_ps, headsT[:, t.ring(-1), p, :], wout[:, p, :], start=(p == 0),
                                        stop=(p == PAIRS - 1))
                    ins.then_inc(s_attn, 1)
                if t.has(-3):
                    pe.wait_ge(s_x2, at(b - 2))
                    after(pe, s_rotT_sb, made(4 * (b + 1) + 1, 4 * B))
                    if isinstance(b, int):
                        turned_copied(b)
                    pe.transpose(turn_ps[:, 0:N], x2[:, t.ring(-3), :], ident[:, :]).then_inc(s_x2T, 1)
                drain(b, 2)
                if t.has(0):
                    scores(b, t.ring(0), 3)
                    transpose_probs(b, 1)
                if t.has(1):
                    transpose_rot(b + 1, 1)
                    project(b + 1, t.ring(1), 4)
                    project(b + 1, t.ring(1), 5)
                if t.has(-2):
                    pe.wait_ge(s_cexp, at(b - 1))
                    after(pe, s_rotT_sb, made(4 * (b + 1) + 2, 4 * B))
                    after(pe, s_x2T_sb, 2 * (b - 2))
                    pe.transpose(turn_ps[:, 0:N], cprobs[:, :], ident[:, :]).then_inc(s_cprobsT, 1)
                drain(b, 3)

            turns(pe, iteration)

            def transpose_sum(k):
                pe.wait_ge(s_acc, at(E * (k + 1)))
                for n in range(TPB):
                    ins = pe.transpose(fin_ps[:, n * N:(n + 1) * N], acc[:, n * N:(n + 1) * N], ident[:, :])
                ins.then_inc(s_fin, 1)

            def add_b2(k):
                after(pe, s_acc, E * (k - 1) + 1)
                pe.matmul(b2_ps, b2_rows[:, :], gatesT[:, bass.ds(at(BLOCK * k), BLOCK)], start=True,
                          stop=True).then_inc(s_b2, 1)

            pe.wait_ge(s_w_lo, B)
            pe.wait_ge(s_x2T_sb, 2 * B)
            add_b2(0)
            first = sum(len(steps) for steps in early_h.values())
            for s in range(first, E * FT):
                step(0, s)
                if s == first:
                    pe.wait_ge(s_y2, B)
                    transpose_gates(1)
                if s == 12:
                    transpose_gates(2)
                if s == 15:
                    pe.wait_ge(s_gatesT_sb, 3)
                    router(1, *ROUTED[1])
                if s == 25:
                    transpose_gates(NBLOCKS - 1)
            pe.wait_ge(s_x2_lo, B)
            pe.wait_ge(s_gatesT_sb, NBLOCKS)
            with pe.Fori(0, NBLOCKS - 1) as i:
                k = Count(i, 1, 1)
                for s in range(E * FT):
                    step(k, s)
                    if s == 4:
                        add_b2(k)
                    if s == 6:
                        transpose_sum(k - 1)
            k = NBLOCKS - 1
            for s in range(E * FT - LAG, E * FT):
                expert_out(k, s)
            for j in range(2):
                pe.wait_ge(s_acc, E * NBLOCKS + j)
                for t in range(HALF):
                    n = HALF * j + t
                    ins = pe.transpose(fin_halves[j][:, t * N:(t + 1) * N], acc[:, n * N:(n + 1) * N], ident[:, :])
                ins.then_inc(s_fin, 1)


HALF = TPB // 2
VECTOR_LOWS, POOL_LOWS = [0, 2, 3], [1, 4, 5]
LAG = 3
CONSTS = 16 * 8
ROUTED = [(0, B - TPB), (B - TPB, B)]
GATE_STEPS = 12
GATE_DIFF = 4

_INS = ['x', 'ctx_1024', 'L0_attn_ln_gamma', 'L0_attn_ln_beta', 'L0_attn_w_qkv', 'L0_attn_w_out', 'L0_attn_b_out',
        'L0_ffn_gate_w', 'L0_ffn_gate_b', 'L0_ffn_w1', 'L0_ffn_b1', 'L0_ffn_w2', 'L0_ffn_b2', 'L0_ffn_ln_g',
        'L0_ffn_ln_b']


def shape_constants():
    import numpy as np
    inv = (1.0 / 10000.0 ** (np.arange(0, HD, 2, dtype=np.float32) / np.float32(HD))).astype(np.float32)
    angle = np.arange(N, dtype=np.float32)[:, None] * inv[None, :]
    sin, cos = np.sin(angle), np.cos(angle)
    table = np.stack([np.concatenate([cos, cos], 1), np.concatenate([sin, -sin], 1)], 1)
    rope = np.stack([table * np.float32(HD ** -0.5), table], 1).astype(np.float32)
    masks = np.zeros((3, 128, 128), np.float32)
    masks[0] = np.eye(128)
    masks[1] = np.triu(np.ones((128, 128)), 1) * -1e10
    masks[2] = np.arange(128)[None, :]
    return {"rope": rope, "masks": masks}


def kernel(**inputs):
    import numpy as _np
    import concourse.bacc as _bacc
    from concourse import mybir as _mybir
    from concourse.bass_utils import run_bass_kernel_spmd as _run

    nc = _bacc.Bacc("TRN2", target_bir_lowering=False, num_devices=1)
    arrays, args = {}, []
    given = [(name, _np.ascontiguousarray(inputs[name])) for name in _INS] + list(shape_constants().items())
    for name, a in given:
        arrays[f"in_{name}_dram"] = a
        args.append(nc.dram_tensor(f"in_{name}_dram", a.shape, _mybir.dt.from_np(a.dtype), kind="ExternalInput").ap())
    args.append(nc.dram_tensor("out_0_dram", (B, N, D), F32, kind="ExternalOutput").ap())
    decoder_kernel(nc, *args)
    r = _run(nc, [arrays], core_ids=[0])
    return r.results[0]["out_0_dram"]
```
